# Optimizing a Trainium2 kernel written in Bass

```python
import numpy as np
import jax
import jax.numpy as jnp

def _softmax(x, axis=-1):
    return jax.nn.softmax(x, axis=axis)
def _gelu(x):
    return jax.nn.gelu(x, approximate=True)
def _silu(x):
    return jax.nn.silu(x)
def _sigmoid(x):
    return jax.nn.sigmoid(x)
def _layernorm(x, axis=-1, eps=1e-5):
    m = jnp.mean(x, axis=axis, keepdims=True)
    v = jnp.var(x, axis=axis, keepdims=True)
    return (x - m) / jnp.sqrt(v + eps)
def _scatter_add(tgt, idx, src, axis=0):
    return tgt.at[idx].add(src)
def _segment_sum(src, seg, n):
    return jax.ops.segment_sum(src, seg, n)

kernel_name = 'mk_adj_preln_d4_adj_128_148598'

def setup_inputs(seed: int = 0):
    np.random.seed(seed)
    _w = jnp.asarray
    def _rec_inputs():
        import jax
        import jax.numpy as jnp
        _gk = jax.random.key(seed)
        x = -0.000929 + 1 * jax.random.normal(jax.random.fold_in(_gk, 1), (8, 2048, 128), jnp.float32)
        _a = jax.random.bernoulli(jax.random.fold_in(_gk, 2), 0.00390625, (8, 2048, 2048))
        adj = _a.astype(jnp.int32)
        return x, adj
    x, adj = _rec_inputs()
    def _L0_gnn_setup():
        import jax, jax.numpy as jnp
        import numpy as np
        ALPHA = 0.2
        NEG = -9000000000000000.0
        key = jax.random.key(seed)
        ks = jax.random.split(key, 6)
        B, N, F, H, D = (16, 512, 128, 8, 32)
        x = jax.random.normal(ks[0], (B, N, F), dtype=jnp.float32)
        adj = jax.random.randint(ks[1], (B, N, N), 0, 2, dtype=jnp.int32)
        W1 = jax.random.normal(ks[2], (H, F, D), dtype=jnp.float32) * (1.414 * (6.0 / (F + D)) ** 0.5)
        a1 = jax.random.normal(ks[3], (H, 2 * D), dtype=jnp.float32) * 0.2
        W2 = jax.random.normal(ks[4], (H * D, F), dtype=jnp.float32) * (1.414 * (6.0 / (H * D + F)) ** 0.5)
        a2 = jax.random.normal(ks[5], (2 * F,), dtype=jnp.float32) * 0.2
        return {'x': x, 'adj': adj, 'W1': W1, 'a1': a1, 'W2': W2, 'a2': a2}
    _L0_gnn_all = _L0_gnn_setup()
    _L0_gnn_in = {k: v for k, v in _L0_gnn_all.items() if k in ('W1', 'a1', 'W2', 'a2', )}
    del _L0_gnn_all

    def _L1_gnn_setup():
        import jax, jax.numpy as jnp
        import numpy as np
        IN_F = 128
        OUT_F = 128
        EPS = 1e-05
        NEG = -1e+30
        key = jax.random.key(seed)
        ks = jax.random.split(key, 8)
        B, N = (2, 1024)
        h = jax.random.normal(ks[0], (B, N, IN_F), dtype=jnp.float32)
        adj = jax.random.randint(ks[1], (B, N, N), 0, 2, dtype=jnp.int32)
        s = (6.0 / (IN_F + OUT_F)) ** 0.5
        W_self = jax.random.uniform(ks[2], (IN_F, OUT_F), jnp.float32, -s, s)
        W_neigh = jax.random.uniform(ks[3], (IN_F, OUT_F), jnp.float32, -s, s)
        b_self = jnp.zeros((OUT_F,), jnp.float32)
        b_neigh = jnp.zeros((OUT_F,), jnp.float32)
        gamma = jnp.ones((OUT_F,), jnp.float32)
        beta = jnp.zeros((OUT_F,), jnp.float32)
        return {'h': h, 'adj': adj, 'W_self': W_self, 'b_self': b_self, 'W_neigh': W_neigh, 'b_neigh': b_neigh, 'gamma': gamma, 'beta': beta}
    _L1_gnn_all = _L1_gnn_setup()
    _L1_gnn_in = {k: v for k, v in _L1_gnn_all.items() if k in ('W_self', 'b_self', 'W_neigh', 'b_neigh', 'gamma', 'beta', )}
    del _L1_gnn_all

    def _L2_gnn_setup():
        import jax, jax.numpy as jnp
        import numpy as np
        B, N, IN_DIM, OUT_DIM, HEADS = (8, 2048, 128, 128, 4)
        HEAD_DIM = OUT_DIM // HEADS
        NEG_BIG = -9000000000000000.0
        key = jax.random.key(seed)
        k1, k2, k3, k4 = jax.random.split(key, 4)
        h = jax.random.normal(k1, (B, N, IN_DIM), dtype=jnp.float32)
        A = jax.random.randint(k2, (B, N, N), 0, 2, dtype=jnp.int32)
        w_bound = (6.0 / (IN_DIM + OUT_DIM)) ** 0.5
        W = jax.random.uniform(k3, (IN_DIM, OUT_DIM), minval=-w_bound, maxval=w_bound, dtype=jnp.float32)
        a_bound = (6.0 / (2 * HEAD_DIM + 1)) ** 0.5
        a = jax.random.uniform(k4, (2 * HEAD_DIM, 1), minval=-a_bound, maxval=a_bound, dtype=jnp.float32)
        return {'h': h, 'A': A, 'W': W, 'a': a}
    _L2_gnn_all = _L2_gnn_setup()
    _L2_gnn_in = {k: v for k, v in _L2_gnn_all.items() if k in ('W', 'a', )}
    del _L2_gnn_all

    def _L3_gnn_setup():
        import jax, jax.numpy as jnp
        import numpy as np
        BATCH, SEQ, D_IN, D_OUT = (32, 1024, 128, 128)
        NEG_SLOPE = 0.1
        key = jax.random.key(seed)
        k1, k2, k3, k4 = jax.random.split(key, 4)
        nodes = jax.random.normal(k1, (BATCH, SEQ, D_IN), dtype=jnp.float32)
        adjacent = jax.random.randint(k2, (BATCH, SEQ, SEQ), 0, 2, dtype=jnp.int32)
        W = jax.random.normal(k3, (D_IN, D_OUT), dtype=jnp.float32) / np.sqrt(D_IN)
        B = jax.random.normal(k4, (D_IN, D_OUT), dtype=jnp.float32) / np.sqrt(D_IN)
        return {'nodes': nodes, 'adjacent': adjacent, 'W': W, 'B': B}
    _L3_gnn_all = _L3_gnn_setup()
    _L3_gnn_in = {k: v for k, v in _L3_gnn_all.items() if k in ('W', 'B', )}
    del _L3_gnn_all

    return {
        "x": x,
        "adj": adj,
        "L0_gnn_W1": _L0_gnn_in["W1"],
        "L0_gnn_a1": _L0_gnn_in["a1"],
        "L0_gnn_W2": _L0_gnn_in["W2"],
        "L0_gnn_a2": _L0_gnn_in["a2"],
        "L1_gnn_W_self": _L1_gnn_in["W_self"],
        "L1_gnn_b_self": _L1_gnn_in["b_self"],
        "L1_gnn_W_neigh": _L1_gnn_in["W_neigh"],
        "L1_gnn_b_neigh": _L1_gnn_in["b_neigh"],
        "L1_gnn_gamma": _L1_gnn_in["gamma"],
        "L1_gnn_beta": _L1_gnn_in["beta"],
        "L2_gnn_W": _L2_gnn_in["W"],
        "L2_gnn_a": _L2_gnn_in["a"],
        "L3_gnn_W": _L3_gnn_in["W"],
        "L3_gnn_B": _L3_gnn_in["B"],
    }

def reference(x, adj, L0_gnn_W1, L0_gnn_a1, L0_gnn_W2, L0_gnn_a2, L1_gnn_W_self, L1_gnn_b_self, L1_gnn_W_neigh, L1_gnn_b_neigh, L1_gnn_gamma, L1_gnn_beta, L2_gnn_W, L2_gnn_a, L3_gnn_W, L3_gnn_B):
    import jax
    import jax.numpy as jnp
    def _L0_gnn_ref(x, adj, W1, a1, W2, a2):
        import jax, jax.numpy as jnp
        import numpy as np
        ALPHA = 0.2
        NEG = -9000000000000000.0
        mask = adj > 0
        h = jnp.einsum('bnf,hfd->bhnd', x, W1)
        D = h.shape[-1]
        f1 = jnp.einsum('bhnd,hd->bhn', h, a1[:, :D])
        f2 = jnp.einsum('bhnd,hd->bhn', h, a1[:, D:])
        e = jax.nn.leaky_relu(f1[..., :, None] + f2[..., None, :], ALPHA)
        e = jnp.where(mask[:, None, :, :], e, NEG)
        att = jax.nn.softmax(e, axis=-1)
        hp = jnp.einsum('bhij,bhjd->bhid', att, h)
        hp = jax.nn.elu(hp)
        B, H, N, Dh = hp.shape
        xc = hp.transpose(0, 2, 1, 3).reshape(B, N, H * Dh)
        h2 = jnp.einsum('bnk,kc->bnc', xc, W2)
        C = h2.shape[-1]
        g1 = jnp.einsum('bnc,c->bn', h2, a2[:C])
        g2 = jnp.einsum('bnc,c->bn', h2, a2[C:])
        e2 = jax.nn.leaky_relu(g1[:, :, None] + g2[:, None, :], ALPHA)
        e2 = jnp.where(mask, e2, NEG)
        att2 = jax.nn.softmax(e2, axis=-1)
        hp2 = jnp.einsum('bij,bjc->bic', att2, h2)
        return jax.nn.elu(hp2) + x

    def _L1_gnn_ref(h, adj, W_self, b_self, W_neigh, b_neigh, gamma, beta):
        import jax, jax.numpy as jnp
        import numpy as np
        IN_F = 128
        OUT_F = 128
        EPS = 1e-05
        NEG = -1e+30
        dtype = h.dtype
        N = adj.shape[-1]
        eye = jnp.eye(N, dtype=dtype)
        adj_ns = adj.astype(dtype) * (1.0 - eye)
        mask = adj_ns > 0
        cand = jnp.where(mask[..., None], h[:, None, :, :], jnp.asarray(NEG, dtype))
        mx = cand.max(axis=2)
        has_neigh = mask.any(axis=-1, keepdims=True)
        neigh_agg = jnp.where(has_neigh, mx, h)
        self_feat = jnp.einsum('bnf,fo->bno', h, W_self) + b_self
        neigh_feat = jnp.einsum('bnf,fo->bno', neigh_agg, W_neigh) + b_neigh
        out = self_feat + neigh_feat
        mu = out.mean(axis=-1, keepdims=True)
        var = out.var(axis=-1, keepdims=True)
        out = (out - mu) * jax.lax.rsqrt(var + EPS) * gamma + beta
        return jax.nn.relu(out)

    def _L2_gnn_ref(h, A, W, a):
        import jax, jax.numpy as jnp
        import numpy as np
        B, N, IN_DIM, OUT_DIM, HEADS = (8, 2048, 128, 128, 4)
        HEAD_DIM = OUT_DIM // HEADS
        NEG_BIG = -9000000000000000.0
        batch, n, _ = h.shape
        Wh = (h @ W).reshape(batch, n, HEADS, HEAD_DIM).transpose(2, 0, 1, 3)
        Wh1 = Wh @ a[:HEAD_DIM, :]
        Wh2 = Wh @ a[HEAD_DIM:, :]
        e = Wh1 + jnp.swapaxes(Wh2, 2, 3)
        e = jnp.where(e > 0, e, 0.2 * e)
        e = jnp.where(A[None] > 0, e, NEG_BIG)
        attn = jax.nn.softmax(e, axis=-1)
        h_prime = attn @ Wh
        h_prime = h_prime.transpose(1, 2, 0, 3).reshape(batch, n, OUT_DIM)
        return h_prime

    def _L3_gnn_ref(nodes, adjacent, W, B):
        import jax, jax.numpy as jnp
        import numpy as np
        BATCH, SEQ, D_IN, D_OUT = (32, 1024, 128, 128)
        NEG_SLOPE = 0.1
        mask = (adjacent != 0).astype(nodes.dtype)
        counts = mask.sum(axis=1)
        pooled = jnp.einsum('boi,bod->bid', mask, nodes)
        pooled = jnp.where(counts[..., None] > 0, pooled / jnp.maximum(counts, 1.0)[..., None], jnp.zeros((), dtype=nodes.dtype))
        updated = nodes @ B + pooled @ W
        return jax.nn.leaky_relu(updated, negative_slope=NEG_SLOPE)

    h = jnp.maximum(_layernorm(x, axis=-1), 0.0)
    x = x + _L0_gnn_ref(h, adj, L0_gnn_W1, L0_gnn_a1, L0_gnn_W2, L0_gnn_a2)
    h = jnp.maximum(_layernorm(x, axis=-1), 0.0)
    x = x + _L1_gnn_ref(h, adj, L1_gnn_W_self, L1_gnn_b_self, L1_gnn_W_neigh, L1_gnn_b_neigh, L1_gnn_gamma, L1_gnn_beta)
    h = jnp.maximum(_layernorm(x, axis=-1), 0.0)
    x = x + _L2_gnn_ref(h, adj, L2_gnn_W, L2_gnn_a)
    h = jnp.maximum(_layernorm(x, axis=-1), 0.0)
    x = x + _L3_gnn_ref(h, adj, L3_gnn_W, L3_gnn_B)
    return x


_drawn_inputs = setup_inputs


def setup_inputs(seed=0):
    import zlib

    import numpy as np

    out = dict(_drawn_inputs(seed))
    spreads = {'L1_gnn_b_self': (0.0, 0.731),
     'L1_gnn_b_neigh': (0.0, 0.7),
     'L1_gnn_gamma': (1.0, 0.2),
     'L1_gnn_beta': (0.0, 0.378)}
    factors = {'L2_gnn_a': 2.821}
    for name, (base, spread) in spreads.items():
        noise = np.random.default_rng([zlib.crc32(name.encode()), seed]).standard_normal(out[name].shape)
        drawn = base * np.exp(spread * noise) if base else spread * noise
        out[name] = jnp.asarray(drawn.astype(out[name].dtype))
    for name, factor in factors.items():
        out[name] = (out[name] * factor).astype(out[name].dtype)
    return out
```

```python
from contextlib import ExitStack

import concourse.bass as bass
from concourse import mybir

ALU = mybir.AluOpType
ACT = mybir.ActivationFunctionType
AX = mybir.AxisListType.X
F32, BF16, F16 = mybir.dt.float32, mybir.dt.bfloat16, mybir.dt.float16
U8, U32, I32 = mybir.dt.uint8, mybir.dt.uint32, mybir.dt.int32

P = 128
EPS = 1e-5
SLOPE = 0.2
SLOPE3 = 0.1
GQ, GD = 40.0, 10.0
KEYS = 8
HALF = KEYS // 2
LOADS = 14


class Layer:

    def __init__(self, name, H, D, KB):
        self.name, self.H, self.D, self.KB = name, H, D, KB
        self.C = D + 1
        self.width = max(self.C, 128)
        self.per_bank = 512 // self.width


def build(nc, x, adj, W1, a1, W2, a2, Wself, bself, Wneigh, bneigh, gamma, beta, WC, aC, W3, B3, out):
    B, N, F = x.shape
    T = N // P
    LA = Layer("gat_heads", W1.shape[0], W1.shape[2], 1)
    LB = Layer("gat_out", 1, F, W1.shape[0] * W1.shape[2] // P)
    LC = Layer("gat_mid", 4, WC.shape[1] // 4, 1)
    HIDDEN = LA.H * LA.D
    KW = N + KEYS
    SP3 = 3 * F + 2

    with ExitStack() as ctx:
        def sb(name, shape, dt=F32):
            return ctx.enter_context(nc.sbuf_tensor(name, shape, dt))

        def sem(name):
            return ctx.enter_context(nc.semaphore(name))

        A = sb("A", [P, T, N], BF16)
        AT = sb("AT", [P, T, N], U8)
        X = sb("X", [P, T, F])
        Hn = sb("Hn", [P, T, F])
        Agg = sb("Agg", [P, T, F])
        WHbuf = sb("WHbuf", [P, T * LA.H * LA.C + LA.width - LA.C])
        xcbuf = sb("xcbuf", [P, T * HIDDEN])
        Pbuf = sb("Pbuf", [P, 2, N])
        Rb = sb("Rb", [P, 2, N])
        hT = sb("hT", [P, 2, 2, P])
        iota = sb("iota", [P, N], F16)
        ident = sb("ident", [P, P])
        identb = sb("identb", [P, P], BF16)
        offdiag = sb("offdiag", [P, P], BF16)
        ones = sb("ones", [P, P])
        before = sb("before", [T, T + 1])
        selfidx = sb("selfidx", [P, T])
        tmpi = sb("tmpi", [P, T], I32)
        shiftq = sb("shiftq", [P, 1])
        shiftd = sb("shiftd", [P, 1])
        eps = sb("eps", [P, 1])
        zero_row = sb("zero_row", [1, F])
        Wf = {}
        for L in (LA, LB, LC):
            Wf[L] = dict(cat=sb(L.name + "_cat", [P, L.KB, L.H * L.D + L.H]),
                         f1=sb(L.name + "_f1", [P, L.KB, L.H]), f2=sb(L.name + "_f2", [P, L.KB, L.H]))
        Wsn = sb("Wsn", [P, 2, F])
        W3s = sb("W3s", [P, 2, F])
        rowsb = sb("rowsb", [P, 4, F])
        deg = sb("deg", [P, T])
        lone = sb("lone", [P, T])
        selfkey = sb("selfkey", [P, T])
        aii = sb("aii", [P, T])
        small = sb("small", [P, 5, T])
        pooled = sb("pooled", [P, 2, F])
        count = sb("count", [P, 2, 1])
        stats = sb("stats", [P, T, 6])
        f2c = sb("f2c", [P, T, 8])
        q = sb("q", [P, T, 8])
        d = sb("d", [P, T, 8])
        hsum = sb("hsum", [P, LA.H * LA.C])
        hpart = sb("hpart", [P, LA.H * LA.C])
        cmax = sb("cmax", [8, 1])
        cdiag = sb("cdiag", [8, 8])
        cb = sb("cb", [P, 8])
        rden = sb("rden", [P, T])
        mdeg = sb("mdeg", [T, 2])
        mdegi = sb("mdegi", [T, 2], I32)
        cumf = sb("cumf", [1, T + 1])
        cum = sb("cum", [1, T + 1], I32)
        base = sb("base", [1, 1])
        keys8 = sb("keys8", [P, KEYS])
        idx = sb("idx", [P, KEYS], U32)

        stage_i32 = Rb[:, :, :].bitcast(I32)
        f1row, f2row = Pbuf[0:8, 0, :], Pbuf[0:8, 1, :]
        xc = xcbuf[:, :].rearrange("p (t c) -> p t c", t=T)
        Dg = xcbuf[:, 0:T * F // 2].bitcast(BF16).rearrange("p (t c) -> p t c", t=T)
        key = xcbuf[:, 0:KW // 2].bitcast(F16)
        G = xcbuf[:, KW // 2:KW // 2 + 2 * (HALF + 1) * F].rearrange("p (s f) -> p s f", f=F)
        PS3 = WHbuf[:, 0:T * SP3 // 2].bitcast(BF16).rearrange("p (t c) -> p t c", t=T)
        Aflat = Agg[:, :, :].rearrange("p t f -> p (t f)")
        Zs = Aflat[:, 0:T * LA.C]
        Es = Aflat[:, T * LA.C:T * (LA.C + LA.D)]
        Pflat = Pbuf[:, :, :].rearrange("p u n -> p (u n)")
        rest = Pbuf[:, 0, :].rearrange("p (t f) -> p t f", t=T)

        def WH(L):
            return WHbuf[:, 0:T * L.H * L.C].rearrange("p (t h c) -> p t h c", t=T, h=L.H)

        ps = ctx.enter_context(nc.psum_tensor("ps", [P, 8, 512], F32))
        psb = ps[:, :, :].rearrange("p b c -> p (b c)").bitcast(BF16).rearrange("p (b c) -> p b c", b=4)

        table = nc.dram_tensor("table", [N + 1, F], F32, kind="Internal").ap()
        rrows = nc.dram_tensor("rrows", [3, 8, N], F32, kind="Internal").ap()

        w_in = sem("w_in")
        w_fold = sem("w_fold")
        cchain = sem("cchain")
        consts = sem("consts")
        ready = sem("ready")
        settled = sem("settled")
        zero_in = sem("zero_in")
        x_in = sem("x_in")
        adj_in = [sem("adj_in0"), sem("adj_in1")]
        cast_done = sem("cast_done")
        at_ps = sem("at_ps")
        at_done = sem("at_done")
        dg_done = sem("dg_done")
        deg_ps = sem("deg_ps")
        cum_ps = sem("cum_ps")
        lv = sem("lv")
        ln = [dict(root=sem(f"ln{k}_root"), st=sem(f"ln{k}_stats"), v=sem(f"ln{k}_chain"), h=sem(f"ln{k}_done")) for k in range(5)]
        S = {L: {k: sem(f"{L.name}_{k}") for k in (
            "T",
            "hT",
            "W",
            "ev",
            "row",
            "v",
            "hs",
            "hsc",
            "cb",
            "exp",
            "rst",
            "rin0", "rin1",
            "p",
            "pe",
            "e",
            "pv",
        )} for L in (LA, LB, LC)}
        tab_in = sem("tab_in")
        keyed = sem("keyed")
        key_pad = sem("key_pad")
        found = sem("found")
        idx_ready = [sem("idx_ready0"), sem("idx_ready1")]
        got = [[sem(f"got{h * HALF + s}") for s in range(HALF)] for h in range(2)]
        reduced = sem("reduced")
        cleared = sem("cleared")
        M = {m: {k: sem(f"{m}_{k}") for k in ("T", "hT", "W", "ev", "y")} for m in ("sage", "pool")}
        part = sem("part")
        rest_done = sem("rest_done")
        ones3 = sem("ones3")
        pool_ps = sem("pool_ps")
        pool_v = sem("pool_v")
        x_done = sem("x_done")
        out_done = sem("out_done")

        LN_CHAIN, PREP_CHAIN, LV_CHAIN, POOL_CHAIN = 7, 8, 11, 4
        POST = {LA: 7, LB: 9, LC: 5}
        ACC_READ = 2
        MINNED = {LA: 5, LB: 6}
        P0 = {LA: 2 * T, LB: 0, LC: 2 * T}

        def plain(eng):
            eng.wait_ge(ready, 1)

        def settle(eng):
            eng.sem_inc(settled, 1)

        class Chain:

            def __init__(self, eng, s, start, total):
                self.eng, self.s, self.start, self.total, self.n = eng, s, start, total, 0

            def __call__(self, ins):
                self.n += 1
                ins.then_inc(self.s, 1)
                plain(self.eng)
                self.eng.wait_ge(self.s, self.start + self.n)

            def end(self):
                assert self.n == self.total, (self.n, self.total)

        block = ctx.enter_context(nc.Block())

        @block.sync
        def _(sp):
            loads = (
                (Wf[LA]["cat"][:, 0, 0:HIDDEN].rearrange("p (h d) -> p h d", h=LA.H), W1.rearrange("h f d -> f h d")),
                (Wf[LB]["cat"][:, :, 0:F], W2.rearrange("(k p) c -> p k c", p=P)),
                (Wf[LC]["cat"][:, 0, 0:F], WC),
                (Wsn[:, 0, :], Wself), (Wsn[:, 1, :], Wneigh), (W3s[:, 0, :], B3), (W3s[:, 1, :], W3),
                (rowsb[:, 0, :], bself.partition_broadcast(P)), (rowsb[:, 1, :], bneigh.partition_broadcast(P)),
                (rowsb[:, 2, :], gamma.partition_broadcast(P)), (rowsb[:, 3, :], beta.partition_broadcast(P)),
                (Pbuf[:, 0, 0:2 * HIDDEN], a1.rearrange("h d -> (h d)").partition_broadcast(P)),
                (Pbuf[:, 1, 0:2 * F], a2.partition_broadcast(P)),
                (Pbuf[:, 1, 512:512 + 2 * LC.D], aC.rearrange("d o -> (d o)").partition_broadcast(P)),
            )
            assert len(loads) == LOADS
            for dst, src in loads:
                sp.dma_start(dst, src).then_inc(w_in, 16)
            sp.wait_ge(ready, 1)
            sp.dma_start(table[0:1, :], zero_row[:, :]).then_inc(zero_in, 16)
            sp.wait_ge(zero_in, 16)
            sp.sem_inc(out_done, 16)

            with sp.Fori(0, B) as b:
                plain(sp)
                sp.wait_ge(out_done, b * 16 + 16)
                settle(sp)
                with sp.Fori(0, T // 2) as tt:
                    for u in range(2):
                        rows = x[bass.ds(b, 1), bass.ds(tt * (2 * P) + u * P, P), :].rearrange("o p f -> (o p) f")
                        sp.dma_start(X[:, bass.ds(tt * 2 + u, 1), :].rearrange("p o f -> p (o f)"), rows).then_inc(x_in, 16)
                        plain(sp)
                        sp.wait_ge(cast_done, b * T + tt * 2 + (u + 1))
                        src = adj[bass.ds(b, 1), bass.ds(tt * (2 * P) + u * P, P), :].rearrange("o p n -> (o p) n")
                        sp.dma_start(stage_i32[:, u, :], src).then_inc(adj_in[u], 16)

                for li, L in enumerate((LA, LB, LC)):
                    s = S[L]
                    if L is LC:
                        plain(sp)
                        sp.wait_ge(ln[1]["h"], (b + 1) * T)
                        sp.dma_start(table[1:N + 1, :].rearrange("(t p) f -> p t f", p=P), Hn[:, :, :]).then_inc(tab_in, 16)
                    plain(sp)
                    sp.wait_ge(s["exp"], (b + 1) * 3)
                    sp.dma_start(rrows[li, 0:L.H, :], f1row[0:L.H, :]).then_inc(s["rst"], 16)
                    plain(sp)
                    sp.wait_ge(s["rst"], b * 16 + 16)
                    settle(sp)
                    if L.H == 1:
                        sp.dma_start(Rb[:, 0, :], rrows[li, 0, :].partition_broadcast(P)).then_inc(s["rin0"], 16)
                    else:
                        with sp.Fori(0, L.H // 2) as hh:
                            for u in range(2):
                                plain(sp)
                                sp.wait_ge(s["p"], (b * L.H + hh * 2 + (u + 1)) * T)
                                src = rrows[li, bass.ds(hh * 2 + u, 1), :].rearrange("o n -> (o n)")
                                sp.dma_start(Rb[:, u, :], src.partition_broadcast(P)).then_inc(s[f"rin{u}"], 16)
                plain(sp)
                sp.wait_ge(x_done, b + 1)
                sp.dma_start(out[bass.ds(b, 1)].rearrange("o (t p) f -> p (o t) f", p=P), X[:, :, :]).then_inc(out_done, 16)
            sp.wait_ge(out_done, B * 16 + 16)

        @block.gpsimd
        def _(pool):
            built = [0]

            def c(ins):
                built[0] += 1
                ins.then_inc(cchain, 1)
                pool.wait_ge(cchain, built[0])

            c(pool.memset(ones[:, :], 1.0))
            c(pool.memset(shiftq[:, :], GQ))
            c(pool.memset(shiftd[:, :], GD))
            c(pool.memset(eps[:, :], EPS))
            c(pool.memset(zero_row[:, :], 0.0))
            c(pool.memset(base[:, :], 0.0))
            c(pool.affine_select(out=ident[:, :], in_=ones[:, :], compare_op=ALU.is_equal, fill=0.0, base=0,
                                 pattern=[[-1, P]], channel_multiplier=1))
            c(pool.affine_select(out=before[:, :], in_=ones[0:T, 0:T + 1], compare_op=ALU.is_gt, fill=0.0, base=0,
                                 pattern=[[1, T + 1]], channel_multiplier=-1))
            c(pool.tensor_copy(identb[:, :], ident[:, :]))
            c(pool.affine_select(out=offdiag[:, :], in_=ones[:, :], compare_op=ALU.not_equal, fill=0.0, base=0,
                                 pattern=[[-1, P]], channel_multiplier=1))
            numbers = Rb[:, 0, :].bitcast(I32)
            c(pool.iota(numbers, [[1, N]], base=1, channel_multiplier=0))
            c(pool.tensor_copy(iota[:, :], numbers))
            c(pool.iota(tmpi[:, :], [[P, T]], base=1, channel_multiplier=1))
            pool.tensor_copy(selfidx[:, :], tmpi[:, :]).then_inc(consts, 1)

            with pool.Fori(0, B) as b:
                plain(pool)
                pool.wait_ge(tab_in, b * 16 + 16)
                plain(pool)
                pool.wait_ge(lv, (b + 1) * LV_CHAIN)
                settle(pool)
                first = pool.value_load(cum[0:1, 0:1], min_val=0, max_val=1 << 20)
                last = pool.value_load(cum[0:1, T:T + 1], min_val=0, max_val=1 << 20)
                with pool.Fori(first, last) as r:
                    for half in range(2):
                        plain(pool)
                        pool.wait_ge(idx_ready[half], r + 1)
                        settle(pool)
                        for s in range(HALF):
                            k = half * HALF + s
                            pool.indirect_dma_start(
                                out=G[:, k + half + 1, :], out_offset=None, in_=table,
                                in_offset=bass.IndirectOffsetOnAxis(ap=idx[:, k:k + 1], axis=0)).then_inc(got[half][s], 16)

        @block.scalar
        def _(act):
            def norm(k, b, src, dst, func):
                plain(act)
                act.wait_ge(ln[k]["v"], b * LN_CHAIN + 5)
                act.activation(small[:, 4, :], small[:, 4, :], ACT.Sqrt, bias=eps[:, 0:1], scale=1.0 / F).then_inc(ln[k]["root"], 1)
                plain(act)
                act.wait_ge(ln[k]["v"], (b + 1) * LN_CHAIN)
                with act.Fori(0, T) as t:
                    act.activation(dst[:, bass.ds(t, 1), :], src[:, bass.ds(t, 1), :], func,
                                   bias=small[:, 1, bass.ds(t, 1)], scale=small[:, 0, bass.ds(t, 1)]).then_inc(ln[k]["h"], 1)

            def prepare(L, b):
                s = S[L]
                with act.Fori(0, T // 2) as tt:
                    for u in range(2):
                        n = b * T + tt * 2 + u
                        plain(act)
                        act.wait_ge(s["T"], n + 1)
                        act.wait_ge(s["W"], n + 1)
                        act.activation(hT[:, u, 0:L.KB, :], ps[:, u, 0:L.KB * P].rearrange("p (k c) -> p k c", k=L.KB),
                                       ACT.Copy).then_inc(s["hT"], 1)
                    for u in range(2):
                        n = b * T + tt * 2 + u
                        plain(act)
                        act.wait_ge(s["W"], n + 3)
                        for k, row in enumerate((f1row, f2row)):
                            act.activation(row[0:L.H, bass.ds(tt * (2 * P) + u * P, P)],
                                           ps[0:L.H, 4 + u, k * P:(k + 1) * P], ACT.Copy).then_inc(s["row"], 1)
                plain(act)
                act.wait_ge(s["hs"], b + 1)
                act.activation(hsum[:, 0:L.H * L.C], ps[:, 6, 0:L.H * L.C], ACT.Copy).then_inc(s["hsc"], 1)
                plain(act)
                act.wait_ge(s["v"], b * PREP_CHAIN + 7)
                act.activation(q[:, :, 0:L.H], f2c[:, :, 0:L.H], ACT.Exp, bias=shiftq[:, 0:1], scale=1 - SLOPE).then_inc(s["exp"], 1)
                act.activation(d[:, :, 0:L.H], f2c[:, :, 0:L.H], ACT.Exp, bias=shiftd[:, 0:1], scale=SLOPE).then_inc(s["exp"], 1)
                act.activation(f1row[0:L.H, :], f2row[0:L.H, :], ACT.Exp, bias=shiftq[0:L.H, 0:1], scale=1.0).then_inc(s["exp"], 1)

            def elu_exp(L, n):
                plain(act)
                act.wait_ge(S[L]["pv"], n * POST[L] + MINNED[L] + 2 * POST[L])
                E = Es if L is LA else xcbuf[:, 0:T * L.D]
                act.activation(E, E, ACT.Exp).then_inc(S[L]["e"], 1)

            def operands(m, b, results):
                with act.Fori(0, T // 2) as tt:
                    for u in range(2):
                        n = b * T + tt * 2 + u
                        plain(act)
                        act.wait_ge(M[m]["T"], n + 1)
                        act.wait_ge(M[m]["W"], n + 1)
                        act.activation(hT[:, u, :, :], ps[:, u, 0:2 * P].rearrange("p (k c) -> p k c", k=2),
                                       ACT.Copy).then_inc(M[m]["hT"], 1)
                    if results:
                        for u in range(2):
                            plain(act)
                            act.wait_ge(M[m]["W"], b * T + tt * 2 + (u + 3))
                            act.activation(Agg[:, bass.ds(tt * 2 + u, 1), :],
                                           ps[:, 2 + u, 0:F].rearrange("p (o f) -> p o f", o=1), ACT.Copy).then_inc(M[m]["ev"], 1)

            act.sem_inc(cast_done, 2)
            for L in (LA, LB, LC):
                act.sem_inc(S[L]["hT"], 2)
                act.sem_inc(S[L]["row"], 4)
            for m in ("sage", "pool"):
                act.sem_inc(M[m]["hT"], 2)
            act.sem_inc(M["pool"]["ev"], 2)
            act.wait_ge(ready, 1)
            with act.Fori(0, B) as b:
                with act.Fori(0, T // 2) as tt:
                    for u in range(2):
                        plain(act)
                        act.wait_ge(adj_in[u], (b * (T // 2) + tt + 1) * 16)
                        act.activation(A[:, bass.ds(tt * 2 + u, 1), :], stage_i32[:, u, :].rearrange("p (o n) -> p o n", o=1),
                                       ACT.Copy, accum_out=deg[:, bass.ds(tt * 2 + u, 1)]).then_inc(cast_done, 1)
                norm(0, b, X, Hn, ACT.Relu)
                prepare(LA, b)
                with act.Fori(0, LA.H) as h:
                    elu_exp(LA, b * LA.H + h)
                prepare(LB, b)
                elu_exp(LB, b)
                norm(1, b, X, Hn, ACT.Relu)
                operands("sage", b, False)
                norm(4, b, Agg, Agg, ACT.Identity)
                norm(2, b, X, Hn, ACT.Relu)
                prepare(LC, b)
                norm(3, b, X, Hn, ACT.Relu)
                plain(act)
                act.wait_ge(ln[3]["h"], (b + 1) * T)
                act.activation(PS3[:, :, 0:F], Hn[:, :, :], ACT.Copy).then_inc(part, 1)
                for k in (1, 2):
                    plain(act)
                    act.wait_ge(rest_done, b * 2 + k)
                    act.activation(PS3[:, :, k * F:(k + 1) * F], rest, ACT.Copy).then_inc(part, 1)
                operands("pool", b, True)

        @block.vector
        def _(dve):
            def statistics(k, b, src):
                settle(dve)
                with dve.Fori(0, T) as t:
                    dve.bn_stats(stats[:, bass.ds(t, 1), :].rearrange("p o c -> p (o c)"),
                                 src[:, bass.ds(t, 1), :].rearrange("p o c -> p (o c)")).then_inc(ln[k]["st"], 1)
                plain(dve)
                dve.wait_ge(ln[k]["st"], (b + 1) * T)
                v = Chain(dve, ln[k]["v"], b * LN_CHAIN, LN_CHAIN)
                mean_e, m2_e, mean_o, m2_o = (stats[:, :, i] for i in (1, 2, 4, 5))
                v(dve.tensor_tensor(small[:, 2, :], mean_e, mean_o, ALU.add))
                v(dve.tensor_tensor(small[:, 3, :], mean_e, mean_o, ALU.subtract))
                v(dve.tensor_tensor(small[:, 4, :], m2_e, m2_o, ALU.add))
                v(dve.scalar_tensor_tensor(small[:, 3, :], small[:, 3, :], F / 4, small[:, 3, :], ALU.mult, ALU.mult))
                v(dve.tensor_tensor(small[:, 4, :], small[:, 4, :], small[:, 3, :], ALU.add))
                plain(dve)
                dve.wait_ge(ln[k]["root"], b + 1)
                v(dve.reciprocal(small[:, 0, :], small[:, 4, :]))
                v(dve.scalar_tensor_tensor(small[:, 1, :], small[:, 2, :], -0.5, small[:, 0, :], ALU.mult, ALU.mult))
                v.end()

            def prepare(L, b):
                s, wh = S[L], WH(L)
                settle(dve)
                with dve.Fori(0, T // 2) as tt:
                    for u in range(2):
                        n = b * T + tt * 2 + u
                        plain(dve)
                        dve.wait_ge(s["W"], n + 3)
                        dve.tensor_copy(wh[:, bass.ds(tt * 2 + u, 1), :, 0:L.D].rearrange("p o h d -> p (o h) d"),
                                        ps[:, 2 + u, 0:L.H * L.D].rearrange("p (h d) -> p h d", h=L.H)).then_inc(s["ev"], 1)
                        dve.tensor_copy(f2c[:, bass.ds(tt * 2 + u, 1), 0:L.H].rearrange("p o h -> p (o h)"),
                                        ps[:, 2 + u, L.H * L.D:L.H * L.D + L.H]).then_inc(s["ev"], 1)
                v = Chain(dve, s["v"], b * PREP_CHAIN, PREP_CHAIN)
                plain(dve)
                dve.wait_ge(s["ev"], (b + 1) * 2 * T + 4)
                v(dve.memset(wh[:, :, :, L.D:L.C], 1.0))
                v(dve.tensor_reduce(hpart[:, 0:L.H * L.C], wh.rearrange("p t h c -> p (h c) t"), AX, ALU.add))
                plain(dve)
                dve.wait_ge(s["row"], (b + 1) * 2 * T + 4)
                v(dve.tensor_reduce(cmax[0:L.H, :], f2row[0:L.H, :], AX, ALU.max))
                v(dve.tensor_scalar(cdiag[0:L.H, 0:L.H], ident[0:L.H, 0:L.H], cmax[0:L.H, 0:1], None, ALU.mult))
                v(dve.tensor_scalar(f1row[0:L.H, :], f1row[0:L.H, :], cmax[0:L.H, 0:1], -(1 - SLOPE), ALU.add, ALU.mult))
                v(dve.tensor_scalar(f2row[0:L.H, :], f1row[0:L.H, :], 0.0, None, ALU.min))
                plain(dve)
                dve.wait_ge(s["cb"], b + 1)
                v(dve.tensor_tensor(f2c[:, :, 0:L.H], f2c[:, :, 0:L.H],
                                    ps[:, 7, 0:L.H].rearrange("p (o h) -> p o h", o=1).broadcast_to([P, T, L.H]), ALU.subtract))
                plain(dve)
                dve.wait_ge(s["exp"], b * 3 + 2)
                v(dve.tensor_tensor(wh, wh, d[:, :, 0:L.H].rearrange("p t (h o) -> p t h o", o=1).broadcast_to([P, T, L.H, L.C]),
                                    ALU.mult))
                v.end()

            def weigh(L, slot, loaded, h, hn, between=None):
                s = S[L]
                plain(dve)
                dve.wait_ge(s[f"rin{slot}"], loaded)
                for jb in range(T):
                    plain(dve)
                    dve.wait_ge(s["pe"], hn * T + (jb + 1))
                    dve.scalar_tensor_tensor(Pbuf[:, jb % 2, :], Rb[:, slot, :], q[:, jb, h], AT[:, jb, :],
                                             ALU.max, ALU.mult).then_inc(s["p"], 1)
                    if jb == 3 and between:
                        between()

            def finish(L, slot, h, hn):
                s, C = S[L], L.C
                v = Chain(dve, s["pv"], (hn + 2) * POST[L], POST[L])
                Z = Pflat[:, 0:T * C] if L is LB else Zs[:, 0:T * C]
                E = (xcbuf[:, 0:T * L.D] if L is LB else Es).rearrange("p (t c) -> p t c", c=L.D)
                zt = Z.rearrange("p (t c) -> p t c", c=C)
                o = zt[:, :, 0:L.D]
                hs = hsum[:, 0:C] if L is LB else hsum[:, bass.ds(h * C, C)]
                plain(dve)
                dve.wait_ge(s["pe"], (hn + 1) * T + 2)
                v(dve.tensor_tensor(zt, lone[:, :].rearrange("p (t o) -> p t o", o=1).broadcast_to([P, T, C]),
                                    hs.rearrange("p (o c) -> p o c", o=1).broadcast_to([P, T, C]), ALU.mult))
                if L is LB:
                    full, w = T // L.per_bank, L.per_bank * C
                    zf = Z[:, 0:full * w].rearrange("p (b c) -> p b c", b=full)
                    v(dve.tensor_tensor(zf, zf, ps[:, 0:full, 0:w], ALU.add))
                    v(dve.tensor_tensor(Z[:, full * w:], Z[:, full * w:], ps[:, full, 0:T * C - full * w], ALU.add))
                else:
                    acc = ps[:, 4 * slot:4 * slot + 4, :].rearrange("p b (t c) -> p (b t) c", c=L.width)[:, :, 0:C]
                    v(dve.tensor_tensor(zt, zt, acc, ALU.add))
                v(dve.reciprocal(rden[:, :], zt[:, :, L.D]))
                v(dve.tensor_tensor(o, o, rden[:, :].rearrange("p (t o) -> p t o", o=1).broadcast_to([P, T, L.D]), ALU.mult))
                if L is LC:
                    xs = X[:, :, bass.ds(h * L.D, L.D)]
                    v(dve.tensor_tensor(xs, xs, o, ALU.add))
                else:
                    v(dve.tensor_scalar(E, o, 0.0, None, ALU.min))
                    plain(dve)
                    dve.wait_ge(s["e"], hn + 1)
                    v(dve.scalar_tensor_tensor(E, o, 0.0, E, ALU.max, ALU.add))
                    if L is LA:
                        v(dve.tensor_scalar(xc[:, :, bass.ds(h * L.D, L.D)], E, -1.0, None, ALU.add))
                    else:
                        v(dve.scalar_tensor_tensor(Hn[:, :, :], E, -1.0, Hn[:, :, :], ALU.add, ALU.add))
                        v(dve.tensor_tensor(X[:, :, :], X[:, :, :], Hn[:, :, :], ALU.add))
                v.end()

            def heads(L, b):
                settle(dve)
                with dve.Fori(0, L.H // 2) as hh:
                    h0, h1 = hh * 2, hh * 2 + 1
                    n0, n1 = b * L.H + hh * 2, b * L.H + hh * 2 + 1
                    loaded = (b * (L.H // 2) + hh + 1) * 16
                    weigh(L, 0, loaded, bass.ds(h0, 1), n0)
                    weigh(L, 1, loaded, bass.ds(h1, 1), n1, between=lambda: finish(L, 0, h0, n0))
                    finish(L, 1, h1, n1)

            def tile_keys(t, n):
                v = Chain(dve, keyed, n * 3, 3)
                v(dve.tensor_tensor(key[:, 0:N], A[:, t, :], iota[:, :], ALU.mult))
                blk = key[:, bass.ds(t * P, P)] if not isinstance(t, int) else key[:, t * P:(t + 1) * P]
                v(dve.tensor_tensor(blk, blk, offdiag[:, :], ALU.mult))
                own = selfkey[:, t:t + 1] if isinstance(t, int) else selfkey[:, bass.ds(t, 1)]
                v(dve.tensor_copy(key[:, N:N + 1], own))
                v.end()
                settle(dve)

            def greatest(r):
                ins = dve.max(keys8[:, :], key[:, :])
                ins.then_inc(found, 1)
                plain(dve)
                dve.wait_ge(found, r * 2 + 1)

            def remove(r):
                dve.match_replace(key[:, :], keys8[:, :], key[:, :], 0.0).then_inc(found, 1)
                plain(dve)
                dve.wait_ge(found, r * 2 + 2)
                settle(dve)

            def reduce(half, n, dst):
                plain(dve)
                for s in range(HALF):
                    dve.wait_ge(got[half][s], n * 16)
                rows = G[:, half * (HALF + 1):(half + 1) * (HALF + 1), :].rearrange("p s f -> p f s")
                dve.tensor_reduce(dst, rows, AX, ALU.max).then_inc(reduced, 1)
                plain(dve)
                dve.wait_ge(reduced, n * 2 + (half + 1))

            def indices(half):
                dve.tensor_copy(idx[:, half * HALF:(half + 1) * HALF], keys8[:, half * HALF:(half + 1) * HALF]
                                ).then_inc(idx_ready[half], 1)

            best = (G[:, 0, :], G[:, HALF + 1, :])

            def rounds(t):
                lo = dve.value_load(cum[0:1, t:t + 1] if isinstance(t, int) else cum[0:1, bass.ds(t, 1)], min_val=0, max_val=1 << 20)
                hi = dve.value_load(cum[0:1, t + 1:t + 2] if isinstance(t, int) else cum[0:1, bass.ds(t + 1, 1)], min_val=0, max_val=1 << 20)
                with dve.Fori(lo + 1, hi) as r:
                    greatest(r)
                    for half in range(2):
                        reduce(half, r, best[1 - half])
                        indices(half)
                    remove(r)
                return hi

            def end_tile(t, n, hi, following):
                reduce(0, hi, best[1])
                if following:
                    indices(0)
                dst = Agg[:, t, :] if isinstance(t, int) else Agg[:, bass.ds(t, 1), :].rearrange("p o f -> p (o f)")
                reduce(1, hi, dst)
                dve.memset(best[0], 0.0).then_inc(cleared, 1)
                plain(dve)
                dve.wait_ge(cleared, n + 1)
                settle(dve)
                if following:
                    indices(1)

            def neighbours(b):
                tile_keys(0, b * T)
                first = dve.value_load(cum[0:1, 0:1], min_val=0, max_val=1 << 20)
                greatest(first)
                indices(0)
                indices(1)
                remove(first)
                with dve.Fori(0, T - 1) as t:
                    hi = rounds(t)
                    tile_keys(t + 1, b * T + t + 1)
                    greatest(hi)
                    end_tile(t, b * T + t, hi, True)
                    remove(hi)
                hi = rounds(T - 1)
                end_tile(T - 1, b * T + T - 1, hi, False)

            dve.wait_ge(consts, 1)
            dve.wait_ge(w_in, LOADS * 16)
            folded = [0]

            def f(ins):
                folded[0] += 1
                ins.then_inc(w_fold, 1)
                dve.wait_ge(w_fold, folded[0])

            prod = Hn[:, :, :].rearrange("p t f -> p (t f)")
            for L, av in ((LA, Pbuf[:, 0, 0:2 * HIDDEN].rearrange("p (h e d) -> p h e d", h=LA.H, e=2)),
                          (LB, Pbuf[:, 1, 0:2 * F].rearrange("p (h e d) -> p h e d", h=1, e=2)),
                          (LC, Pbuf[:, 1, 512:512 + 2 * LC.D].rearrange("p (h e d) -> p h e d", h=1, e=2))):
                w = Wf[L]
                for k in range(L.KB):
                    for e, dst in ((0, w["f1"]), (1, w["f2"])):
                        wv = w["cat"][:, k, 0:L.H * L.D].rearrange("p (h d) -> p h d", h=L.H)
                        pv = prod[:, 0:L.H * L.D].rearrange("p (h d) -> p h d", h=L.H)
                        vec = av[:, :, e, :] if L is not LC else av[:, 0:1, e, :].broadcast_to([P, L.H, L.D])
                        f(dve.tensor_tensor(pv, wv, vec, ALU.mult))
                        f(dve.tensor_reduce(dst[:, k, :], pv, AX, ALU.add))
                    f(dve.tensor_copy(w["cat"][:, k, L.H * L.D:], w["f2"][:, k, :]))
            f(dve.tensor_tensor(rowsb[:, 0, :], rowsb[:, 0, :], rowsb[:, 1, :], ALU.add))
            f(dve.memset(WHbuf[:, T * LA.H * LA.C:], 0.0))
            for L in (LA, LB, LC):
                dve.sem_inc(S[L]["ev"], 4)
                dve.sem_inc(S[L]["pv"], 2 * POST[L])
                if P0[L]:
                    dve.sem_inc(S[L]["p"], P0[L])
            dve.sem_inc(at_done, 2)
            dve.sem_inc(reduced, 2)
            dve.sem_inc(M["sage"]["ev"], 2)
            dve.sem_inc(pool_v, 2 * POOL_CHAIN)
            dve.memset(keys8[:, :], 0.0).then_inc(ready, 1)
            dve.wait_ge(ready, 1)

            with dve.Fori(0, B) as b:
                with dve.Fori(0, T // 2) as tt:
                    for u in range(2):
                        n = b * T + tt * 2 + u
                        plain(dve)
                        dve.wait_ge(at_ps, n + 1)
                        dve.tensor_copy(AT[:, :, bass.ds(tt * (2 * P) + u * P, P)],
                                        psb[:, u, :].rearrange("p (j i) -> p j i", j=T)).then_inc(at_done, 1)
                        dve.tensor_tensor(Dg[:, bass.ds(tt * 2 + u, 1), :].rearrange("p o c -> p (o c)"),
                                          A[:, bass.ds(tt * 2 + u, 1), bass.ds(tt * (2 * P) + u * P, P)].rearrange("p o c -> p (o c)"),
                                          identb[:, :], ALU.mult).then_inc(dg_done, 1)
                v = Chain(dve, lv, b * LV_CHAIN, LV_CHAIN)
                plain(dve)
                dve.wait_ge(dg_done, (b + 1) * T)
                v(dve.tensor_reduce(aii[:, :], Dg, AX, ALU.add))
                v(dve.tensor_scalar(lone[:, :], deg[:, :], 0.0, None, ALU.is_equal))
                v(dve.tensor_tensor(aii[:, :], deg[:, :], aii[:, :], ALU.subtract))
                v(dve.scalar_tensor_tensor(selfkey[:, :], aii[:, :], 0.0, selfidx[:, :], ALU.is_equal, ALU.mult))
                plain(dve)
                dve.wait_ge(deg_ps, b + 1)
                v(dve.tensor_reduce(mdeg[:, 0:1], ps[0:T, 4, 0:P], AX, ALU.max))
                v(dve.tensor_scalar(mdegi[:, 0:1], mdeg[:, 0:1], float(KEYS - 1), None, ALU.add))
                v(dve.tensor_scalar(mdegi[:, 1:2], mdegi[:, 0:1], 3, None, ALU.arith_shift_right))
                v(dve.tensor_scalar(mdeg[:, 1:2], mdegi[:, 1:2], 2.0, None, ALU.max))
                plain(dve)
                dve.wait_ge(cum_ps, b + 1)
                v(dve.tensor_scalar(cumf[:, :], ps[0:1, 5, 0:T + 1], base[:, 0:1], None, ALU.add))
                v(dve.tensor_copy(cum[:, :], cumf[:, :]))
                v(dve.tensor_copy(base[:, :], cumf[:, T:T + 1]))
                v.end()

                plain(dve)
                dve.wait_ge(x_in, (b + 1) * T * 16)
                statistics(0, b, X)
                prepare(LA, b)
                heads(LA, b)
                prepare(LB, b)
                weigh(LB, 0, (b + 1) * 16, slice(0, 1), b)
                finish(LB, 0, 0, b)

                statistics(1, b, X)
                dve.memset(key[:, N:KW], 0.0).then_inc(key_pad, 1)
                dve.memset(best[0], 0.0).then_inc(key_pad, 1)
                plain(dve)
                dve.wait_ge(key_pad, b * 2 + 2)
                neighbours(b)
                with dve.Fori(0, T // 2) as tt:
                    for u in range(2):
                        plain(dve)
                        dve.wait_ge(M["sage"]["W"], b * T + tt * 2 + (u + 3))
                        dve.tensor_tensor(Agg[:, bass.ds(tt * 2 + u, 1), :].rearrange("p o f -> p (o f)"), ps[:, 2 + u, 0:F],
                                          rowsb[:, 0, :], ALU.add).then_inc(M["sage"]["ev"], 1)
                plain(dve)
                dve.wait_ge(M["sage"]["ev"], (b + 1) * T + 2)
                statistics(4, b, Agg)
                v = Chain(dve, M["sage"]["y"], b * 3, 3)
                plain(dve)
                dve.wait_ge(ln[4]["h"], (b + 1) * T)
                for op, row in ((ALU.mult, 2), (ALU.add, 3)):
                    v(dve.tensor_tensor(Agg[:, :, :], Agg[:, :, :],
                                        rowsb[:, row:row + 1, :].broadcast_to([P, T, F]), op))
                v(dve.scalar_tensor_tensor(X[:, :, :], Agg[:, :, :], 0.0, X[:, :, :], ALU.max, ALU.add))
                v.end()

                statistics(2, b, X)
                prepare(LC, b)
                heads(LC, b)

                statistics(3, b, X)
                dve.memset(PS3[:, :, 3 * F:SP3], 1.0).then_inc(ones3, 1)
                plain(dve)
                dve.wait_ge(part, b * 3 + 1)
                dve.tensor_tensor(rest, Hn[:, :, :], PS3[:, :, 0:F], ALU.subtract).then_inc(rest_done, 1)
                plain(dve)
                dve.wait_ge(part, b * 3 + 2)
                dve.tensor_tensor(rest, rest, PS3[:, :, F:2 * F], ALU.subtract).then_inc(rest_done, 1)
                with dve.Fori(0, T // 2) as tt:
                    for u in range(2):
                        n = b * T + tt * 2 + u
                        plain(dve)
                        dve.wait_ge(pool_ps, n + 1)
                        v = Chain(dve, pool_v, (n + 2) * POOL_CHAIN, POOL_CHAIN)
                        v(dve.tensor_scalar(count[:, u, :], ps[:, 4 + u, 3 * F:3 * F + 1], 1.0, None, ALU.max))
                        v(dve.reciprocal(count[:, u, :], count[:, u, :]))
                        v(dve.tensor_reduce(pooled[:, u, :], ps[:, 4 + u, 0:3 * F].rearrange("p (k f) -> p f k", k=3), AX, ALU.add))
                        v(dve.tensor_scalar(pooled[:, u, :], pooled[:, u, :], count[:, u, :], None, ALU.mult))
                        v.end()
                v = Chain(dve, M["pool"]["y"], b, 1)
                plain(dve)
                dve.wait_ge(M["pool"]["ev"], (b + 1) * T + 2)
                v(dve.scalar_tensor_tensor(Agg[:, :, :], Agg[:, :, :], SLOPE3, Agg[:, :, :], ALU.mult, ALU.max))
                dve.tensor_tensor(X[:, :, :], X[:, :, :], Agg[:, :, :], ALU.add).then_inc(x_done, 1)

        @block.tensor
        def _(pe):
            def prepare(L, b, source, arrived):
                s, w = S[L], Wf[L]
                W = L.H * L.D + L.H
                if not arrived:
                    plain(pe)
                    pe.wait_ge(S[LA]["pv"], ((b + 1) * LA.H + 2) * POST[LA])
                for tt in range(T // 2):
                    for u in range(2):
                        n = b * T + tt * 2 + u
                        plain(pe)
                        if arrived:
                            pe.wait_ge(arrived, n + 1)
                        pe.wait_ge(s["hT"], n + 1)
                        for k in range(L.KB):
                            ins = pe.transpose(ps[:, u, k * P:(k + 1) * P],
                                               source[:, tt * 2 + u, k * P:(k + 1) * P],
                                               ident[:, :])
                        ins.then_inc(s["T"], 1)
                    for u in range(2):
                        n = b * T + tt * 2 + u
                        plain(pe)
                        pe.wait_ge(s["hT"], n + 3)
                        pe.wait_ge(s["ev"], n * 2 + 2)
                        pe.wait_ge(s["row"], n * 2 + 2)
                        for k in range(L.KB):
                            pe.matmul(ps[:, 2 + u, 0:W], hT[:, u, k, :], w["cat"][:, k, :], start=k == 0, stop=k == L.KB - 1)
                        for e, wf in enumerate((w["f1"], w["f2"])):
                            for k in range(L.KB):
                                ins = pe.matmul(ps[0:L.H, 4 + u, e * P:(e + 1) * P], wf[:, k, :], hT[:, u, k, :],
                                                start=k == 0, stop=k == L.KB - 1)
                        ins.then_inc(s["W"], 1)
                plain(pe)
                pe.wait_ge(s["v"], b * PREP_CHAIN + 2)
                pe.matmul(ps[:, 6, 0:L.H * L.C], ones[:, :], hpart[:, 0:L.H * L.C], start=True, stop=True).then_inc(s["hs"], 1)
                plain(pe)
                pe.wait_ge(s["v"], b * PREP_CHAIN + 4)
                pe.matmul(ps[:, 7, 0:L.H], ones[0:L.H, :], cdiag[0:L.H, 0:L.H], start=True, stop=True).then_inc(s["cb"], 1)

            def sums(L, bank, h, hn):
                s = S[L]
                if L is not LB:
                    plain(pe)
                    pe.wait_ge(s["pv"], hn * POST[L] + ACC_READ)
                for jb in range(T):
                    plain(pe)
                    pe.wait_ge(s["p"], hn * T + (jb + 1 + P0[L]))
                    rhs = WHbuf[:, bass.ds(h * L.C + jb * L.H * L.C, L.width)]
                    for i in range(T):
                        c0 = i % L.per_bank * L.width
                        ins = pe.matmul(ps[:, bank + i // L.per_bank, c0:c0 + L.width], Pbuf[:, jb % 2, i * P:(i + 1) * P], rhs,
                                        start=(jb == 0 and i % L.per_bank == 0), stop=(jb == T - 1), skip_group_check=True)
                    ins.then_inc(s["pe"], 1)

            def heads(L, b):
                plain(pe)
                pe.wait_ge(S[L]["v"], (b + 1) * PREP_CHAIN)
                settle(pe)
                with pe.Fori(0, L.H // 2) as hh:
                    for u in range(2):
                        sums(L, 4 * u, hh * 2 + u, b * L.H + hh * 2 + u)

            def square(m, b, second, arrived, weights):
                s = M[m]
                for tt in range(T // 2):
                    if m == "pool":
                        for u in range(2):
                            n = b * T + tt * 2 + u
                            plain(pe)
                            pe.wait_ge(pool_v, n * POOL_CHAIN + POOL_CHAIN)
                            for k in range(T):
                                ins = pe.matmul(ps[:, 4 + u, 0:3 * F + 1],
                                                A[:, k, (tt * 2 + u) * P:(tt * 2 + u + 1) * P],
                                                PS3[:, k, 0:3 * F + 1], start=k == 0, stop=k == T - 1)
                            ins.then_inc(pool_ps, 1)
                    for u in range(2):
                        n = b * T + tt * 2 + u
                        plain(pe)
                        pe.wait_ge(s["hT"], n + 1)
                        if m == "pool":
                            pe.wait_ge(pool_v, (n + 3) * POOL_CHAIN)
                        pe.transpose(ps[:, u, 0:P], Hn[:, tt * 2 + u, :], ident[:, :])
                        sec = pooled[:, u, :] if m == "pool" else Agg[:, tt * 2 + u, :]
                        pe.transpose(ps[:, u, P:2 * P], sec, ident[:, :]).then_inc(s["T"], 1)
                    for u in range(2):
                        n = b * T + tt * 2 + u
                        plain(pe)
                        pe.wait_ge(s["hT"], n + 3)
                        pe.wait_ge(s["ev"], n + 1)
                        for k in range(2):
                            ins = pe.matmul(ps[:, 2 + u, 0:F], hT[:, u, k, :], weights[:, k, :], start=k == 0, stop=k == 1)
                        ins.then_inc(s["W"], 1)

            for L in (LA, LB, LC):
                pe.sem_inc(S[L]["W"], 2)
                pe.sem_inc(S[L]["pe"], 2)
            for m in ("sage", "pool"):
                pe.sem_inc(M[m]["W"], 2)
            pe.wait_ge(ready, 1)
            with pe.Fori(0, B) as b:
                with pe.Fori(0, T // 2) as tt:
                    for u in range(2):
                        n = b * T + tt * 2 + u
                        plain(pe)
                        pe.wait_ge(cast_done, n + 3)
                        pe.wait_ge(at_done, n + 1)
                        for jb in range(T):
                            ins = pe.transpose(psb[:, u, jb * P:(jb + 1) * P],
                                               A[:, bass.ds(tt * 2 + u, 1), jb * P:(jb + 1) * P].rearrange("p o c -> p (o c)"),
                                               identb[:, :])
                        ins.then_inc(at_ps, 1)
                pe.transpose(ps[0:T, 4, 0:P], deg[:, :], ident[:, :]).then_inc(deg_ps, 1)
                plain(pe)
                pe.wait_ge(lv, b * LV_CHAIN + 8)
                settle(pe)
                pe.matmul(ps[0:1, 5, 0:T + 1], mdeg[:, 1:2], before[:, :], start=True, stop=True).then_inc(cum_ps, 1)

                prepare(LA, b, Hn, ln[0]["h"])
                heads(LA, b)
                prepare(LB, b, xc, None)
                plain(pe)
                pe.wait_ge(S[LB]["v"], (b + 1) * PREP_CHAIN)
                sums(LB, 0, 0, b)
                plain(pe)
                pe.wait_ge(cleared, (b + 1) * T)
                square("sage", b, Agg, None, Wsn)
                prepare(LC, b, Hn, ln[2]["h"])
                heads(LC, b)
                plain(pe)
                pe.wait_ge(part, (b + 1) * 3)
                pe.wait_ge(ones3, b + 1)
                square("pool", b, None, None, W3s)


_INS = ["x", "adj", "L0_gnn_W1", "L0_gnn_a1", "L0_gnn_W2", "L0_gnn_a2", "L1_gnn_W_self", "L1_gnn_b_self", "L1_gnn_W_neigh",
        "L1_gnn_b_neigh", "L1_gnn_gamma", "L1_gnn_beta", "L2_gnn_W", "L2_gnn_a", "L3_gnn_W", "L3_gnn_B"]


def kernel(**inputs):
    import concourse.bacc as bacc
    import numpy as np
    from concourse.bass_utils import run_bass_kernel_spmd

    nc = bacc.Bacc("TRN2", target_bir_lowering=False, num_devices=1)
    arrays, args = {}, []
    for name in _INS:
        a = np.ascontiguousarray(inputs[name])
        arrays["in_" + name] = a
        args.append(nc.dram_tensor("in_" + name, a.shape, mybir.dt.from_np(a.dtype), kind="ExternalInput").ap())
    out = nc.dram_tensor("out", inputs["x"].shape, F32, kind="ExternalOutput").ap()
    build(nc, *args, out)
    r = run_bass_kernel_spmd(nc, [arrays], core_ids=[0])
    return r.results[0]["out"]
```

```python
from contextlib import ExitStack

import concourse.bass as bass
from concourse import mybir

ALU = mybir.AluOpType
ACT = mybir.ActivationFunctionType
AX = mybir.AxisListType.X
F8 = mybir.dt.float8e4
F32, BF16, F16 = mybir.dt.float32, mybir.dt.bfloat16, mybir.dt.float16
U8, U32, I32 = mybir.dt.uint8, mybir.dt.uint32, mybir.dt.int32

P = 128
EPS = 1e-5
SLOPE = 0.2
SLOPE3 = 0.1
GQ, GD = 40.0, 10.0
KEYS = 8
ONE8 = 56
LOADS = 14


class Layer:

    def __init__(self, name, H, D, KB):
        self.name, self.H, self.D, self.KB = name, H, D, KB
        self.C = D + 1
        self.width = max(self.C, 128)
        self.per_bank = 512 // self.width


def build(nc, x, adj, W1, a1, W2, a2, Wself, bself, Wneigh, bneigh, gamma, beta, WC, aC, W3, B3, out):
    B, N, F = x.shape
    T = N // P
    LA = Layer("gat_heads", W1.shape[0], W1.shape[2], 1)
    LB = Layer("gat_out", 1, F, W1.shape[0] * W1.shape[2] // P)
    LC = Layer("gat_mid", 4, WC.shape[1] // 4, 1)
    HIDDEN = LA.H * LA.D
    KW = N + KEYS
    SP3 = 3 * F + 2
    ROUNDS = B * T * N // KEYS
    SHARE = 2 * T // LA.H
    LIST_ALL, LIST_LA, LIST_LC = (0, 4), (0, 2), (LA.H + 1, 3)
    LIST_LB, LIST_L3 = LA.H, T - 1
    END_AT = 3
    assert LIST_LC[0] + LC.H // 2 * LIST_LC[1] == LIST_L3 and LA.H // 2 * LIST_ALL[1] == T

    with ExitStack() as ctx:
        def sb(name, shape, dt=F32):
            return ctx.enter_context(nc.sbuf_tensor(name, shape, dt))

        def sem(name):
            return ctx.enter_context(nc.semaphore(name))

        A = sb("A", [P, T, N], U8)
        AT = sb("AT", [P, T, N], U8)
        X = sb("X", [P, T, F])
        Hn = sb("Hn", [P, T, F])
        X2 = sb("X2", [P, T, F])
        Hn2 = sb("Hn2", [P, T, F])
        Agg = sb("Agg", [P, T, F])
        best = sb("best", [P, KEYS, F])
        G = sb("G", [P, KEYS, F])
        idx = sb("idx", [P, 2, KEYS], U32)
        key = sb("key", [P, KW], F16)
        Zs = sb("Zs", [P, T * LA.C])[:, :]
        Es = sb("Es", [P, T * LA.D])[:, :]
        WHbuf = sb("WHbuf", [P, T * LA.H * LA.C + LA.width - LA.C])
        xcbuf = sb("xcbuf", [P, T * HIDDEN])
        Pbuf = sb("Pbuf", [P, 2, N])
        Rb = sb("Rb", [P, 2, N])
        hT = sb("hT", [P, 2, 2, P])
        iota = sb("iota", [P, N], F16)
        ident = sb("ident", [P, P])
        identb = sb("identb", [P, P], BF16)
        offdiag = sb("offdiag", [P, P], BF16)
        ones = sb("ones", [P, P])
        before = sb("before", [T, T + 1])
        selfidx = sb("selfidx", [P, T])
        tmpi = sb("tmpi", [P, T], I32)
        shiftq = sb("shiftq", [P, 1])
        shiftd = sb("shiftd", [P, 1])
        eps = sb("eps", [P, 1])
        zero_row = sb("zero_row", [1, F])
        Wf = {}
        for L in (LA, LB, LC):
            Wf[L] = dict(cat=sb(L.name + "_cat", [P, L.KB, L.H * L.D + L.H]),
                         f1=sb(L.name + "_f1", [P, L.KB, L.H]), f2=sb(L.name + "_f2", [P, L.KB, L.H]))
        Wsn = sb("Wsn", [P, 2, F])
        W3s = sb("W3s", [P, 2, F])
        rowsb = sb("rowsb", [P, 4, F])
        deg = sb("deg", [P, T])
        lone = sb("lone", [P, T])
        lone_before = sb("lone_before", [P, T])
        selfkey = sb("selfkey", [P, T])
        aii = sb("aii", [P, T])
        small = sb("small", [P, 5, T])
        pooled = sb("pooled", [P, 2, F])
        count = sb("count", [P, 2, 1])
        stats = sb("stats", [P, T, 6])
        f2c = sb("f2c", [P, T, 8])
        q = sb("q", [P, T, 8])
        d = sb("d", [P, T, 8])
        hsum = sb("hsum", [P, LA.H * LA.C])
        hpart = sb("hpart", [P, LA.H * LA.C])
        cmax = sb("cmax", [8, 1])
        cdiag = sb("cdiag", [8, 8])
        cb = sb("cb", [P, 8])
        rden = sb("rden", [P, T])
        mdeg = sb("mdeg", [T, 2])
        mdegi = sb("mdegi", [T, 2], I32)
        cumf = sb("cumf", [1, T + 1])
        cum = sb("cum", [1, B * (T + 1)], I32)
        base = sb("base", [1, 1])
        keys8 = sb("keys8", [P, KEYS])
        found_idx = sb("found_idx", [P, KEYS], U32)

        stage_i32 = Rb[:, :, :].bitcast(I32)
        f1row, f2row = Pbuf[0:8, 0, :], Pbuf[0:8, 1, :]
        xc = xcbuf[:, :].rearrange("p (t c) -> p t c", t=T)
        Dg = xcbuf[:, T * F:T * F + T * F // 2].bitcast(BF16).rearrange("p (t c) -> p t c", t=T)
        stage_bf = Pbuf[:, 0, :].bitcast(BF16).rearrange("p (u n) -> p u n", u=2)
        PS3 = WHbuf[:, 0:T * SP3 // 2].bitcast(BF16).rearrange("p (t c) -> p t c", t=T)
        A8 = AT[:, :, :].bitcast(F8)
        Y = xcbuf[:, 0:T * F].rearrange("p (t f) -> p t f", t=T)
        Pflat = Pbuf[:, :, :].rearrange("p u n -> p (u n)")
        rest = Pbuf[:, 0, :].rearrange("p (t f) -> p t f", t=T)

        tiles_P = {L: [Pbuf[:, 0, :], Pbuf[:, 1, :]] + [buffer[:, :, :].rearrange("p t f -> p (t f)") for buffer in spare]
                   for L, spare in ((LA, (Hn2, X2)), (LB, ()), (LC, (Hn2, X)))}
        free_P = {L: len(tiles_P[L]) for L in tiles_P}

        def WH(L):
            return WHbuf[:, 0:T * L.H * L.C].rearrange("p (t h c) -> p t h c", t=T, h=L.H)

        ps = ctx.enter_context(nc.psum_tensor("ps", [P, 8, 512], F32))
        psb = ps[:, :, :].rearrange("p b c -> p (b c)").bitcast(BF16).rearrange("p (b c) -> p b c", b=4)

        table = nc.dram_tensor("table", [N + 1, F], F32, kind="Internal").ap()
        x1 = nc.dram_tensor("x1", [B, P, T * F], F32, kind="Internal").ap()
        h1 = nc.dram_tensor("h1", [B, P, T * F], F32, kind="Internal").ap()
        bytes_A = nc.dram_tensor("bytes_A", [B * T, P, N], U8, kind="Internal").ap()
        bytes_AT = nc.dram_tensor("bytes_AT", [B * T, P, N], U8, kind="Internal").ap()
        lists = nc.dram_tensor("lists", [ROUNDS + 1, P, KEYS], U32, kind="Internal").ap()
        rrows = nc.dram_tensor("rrows", [3, 8, N], F32, kind="Internal").ap()

        w_in = sem("w_in")
        w_fold = sem("w_fold")
        cchain = sem("cchain")
        consts = sem("consts")
        ready = sem("ready")
        settled = sem("settled")
        zero_in = sem("zero_in")
        x_in = sem("x_in")
        x1_out = sem("x1_out")
        bytes_out = sem("bytes_out")
        x1_in = sem("x1_in")
        A_in = sem("A_in")
        AT_in = sem("AT_in")
        adj_in = [sem("adj_in0"), sem("adj_in1")]
        cast_done = sem("cast_done")
        bf_done = sem("bf_done")
        at_ps = sem("at_ps")
        at_done = sem("at_done")
        dg_done = sem("dg_done")
        deg_ps = sem("deg_ps")
        cum_ps = sem("cum_ps")
        lv = sem("lv")
        ln = [dict(root=sem(f"ln{k}_root"), st=sem(f"ln{k}_stats"), v=sem(f"ln{k}_chain"), h=sem(f"ln{k}_done")) for k in range(5)]
        S = {L: {k: sem(f"{L.name}_{k}") for k in (
            "T",
            "hT",
            "W",
            "ev",
            "row",
            "v",
            "hs",
            "hsc",
            "cb",
            "exp",
            "rst",
            "rin0", "rin1",
            "p",
            "pe",
            "e",
            "pv",
        )} for L in (LA, LB, LC)}
        tab_in = sem("tab_in")
        keyed = sem("keyed")
        found = sem("found")
        removed = sem("removed")
        idx_ready = sem("idx_ready")
        list_in = sem("list_in")
        idx_in = sem("idx_in")
        got = [sem(f"got{s}") for s in range(KEYS)]
        merged = sem("merged")
        tree = sem("tree")
        maxima = sem("maxima")
        M = {m: {k: sem(f"{m}_{k}") for k in ("T", "hT", "W", "ev", "y")} for m in ("sage", "pool")}
        part = sem("part")
        rest_done = sem("rest_done")
        ones3 = sem("ones3")
        pool_ps = sem("pool_ps")
        pool_v = sem("pool_v")
        x_done = sem("x_done")
        out_done = sem("out_done")

        LN_CHAIN, PREP_CHAIN, LV_CHAIN, POOL_CHAIN, TREE = 7, 8, 12, 4, 10
        POST = {LA: 7, LB: 9, LC: 5}
        ACC_READ = 2
        MINNED = {LA: 5, LB: 6}
        P0 = {LA: 2 * T, LB: 0, LC: 2 * T}

        def plain(eng):
            eng.wait_ge(ready, 1)

        def settle(eng):
            eng.sem_inc(settled, 1)

        class Chain:

            def __init__(self, eng, s, start, total):
                self.eng, self.s, self.start, self.total, self.n = eng, s, start, total, 0

            def __call__(self, ins):
                self.n += 1
                ins.then_inc(self.s, 1)
                plain(self.eng)
                self.eng.wait_ge(self.s, self.start + self.n)

            def end(self):
                assert self.n == self.total, (self.n, self.total)

        def pipeline(eng, load, first, second, last_layer):
            load(0, True)
            first(0, True)
            if B > 1:
                load(1, False)
                first(1, False)
            if B > 2:
                with eng.Fori(0, B - 2) as b:
                    second(b, False)
                    last_layer(b, b + 2, False)
                    first(b + 2, False)
            if B > 1:
                second(B - 2, False)
                last_layer(B - 2, None, False)
            second(B - 1, True)
            last_layer(B - 1, None, True)

        block = ctx.enter_context(nc.Block())

        @block.sync
        def _(sp):
            loads = (
                (Wf[LA]["cat"][:, 0, 0:HIDDEN].rearrange("p (h d) -> p h d", h=LA.H), W1.rearrange("h f d -> f h d")),
                (Wf[LB]["cat"][:, :, 0:F], W2.rearrange("(k p) c -> p k c", p=P)),
                (Wf[LC]["cat"][:, 0, 0:F], WC),
                (Wsn[:, 0, :], Wself), (Wsn[:, 1, :], Wneigh), (W3s[:, 0, :], B3), (W3s[:, 1, :], W3),
                (rowsb[:, 0, :], bself.partition_broadcast(P)), (rowsb[:, 1, :], bneigh.partition_broadcast(P)),
                (rowsb[:, 2, :], gamma.partition_broadcast(P)), (rowsb[:, 3, :], beta.partition_broadcast(P)),
                (Pbuf[:, 0, 0:2 * HIDDEN], a1.rearrange("h d -> (h d)").partition_broadcast(P)),
                (Pbuf[:, 1, 0:2 * F], a2.partition_broadcast(P)),
                (Pbuf[:, 1, 512:512 + 2 * LC.D], aC.rearrange("d o -> (d o)").partition_broadcast(P)),
            )
            assert len(loads) == LOADS
            for dst, src in loads:
                sp.dma_start(dst, src).then_inc(w_in, 16)
            sp.wait_ge(ready, 1)
            sp.dma_start(table[0:1, :], zero_row[:, :]).then_inc(zero_in, 16)
            sp.wait_ge(zero_in, 16)

            def of(array, n):
                return array[bass.ds(n, 1)].rearrange("o p c -> (o p) c")

            def tile_of(buffer, t):
                return buffer[:, bass.ds(t, 1), :].rearrange("p o c -> p (o c)")

            def flat(buffer):
                return buffer[:, :, :].rearrange("p t f -> p (t f)")

            def exponentials(L, li, b):
                s = S[L]
                plain(sp)
                sp.wait_ge(s["exp"], b * 3 + 1)
                sp.dma_start(rrows[li, 0:L.H, :], f1row[0:L.H, :]).then_inc(s["rst"], 16)
                plain(sp)
                sp.wait_ge(s["rst"], b * 16 + 16)
                settle(sp)

            def head_rows(L, li, b, hh):
                s = S[L]
                for u in range(2):
                    plain(sp)
                    sp.wait_ge(s["p"], (b * L.H + hh * 2 + (u + 1)) * T)
                    src = rrows[li, bass.ds(hh * 2 + u, 1), :].rearrange("o n -> (o n)")
                    sp.dma_start(Rb[:, u, :], src.partition_broadcast(P)).then_inc(s[f"rin{u}"], 16)

            def load(b, alone):
                with sp.Fori(0, T // 2) as tt:
                    for u in range(2):
                        rows = x[bass.ds(b, 1), bass.ds(tt * (2 * P) + u * P, P), :].rearrange("o p f -> (o p) f")
                        sp.dma_start(tile_of(X, tt * 2 + u), rows).then_inc(x_in, 16)
                        plain(sp)
                        sp.wait_ge(cast_done, b * T + tt * 2 + (u + 1))
                        src = adj[bass.ds(b, 1), bass.ds(tt * (2 * P) + u * P, P), :].rearrange("o p n -> (o p) n")
                        sp.dma_start(stage_i32[:, u, :], src).then_inc(adj_in[u], 16)

            def first(b, alone):
                exponentials(LA, 0, b)
                plain(sp)
                sp.wait_ge(cast_done, b * T + (T + 2))
                sp.wait_ge(at_done, b * T + (T + 2))
                settle(sp)
                with sp.Fori(0, LA.H // 2) as hh:
                    head_rows(LA, 0, b, hh)
                    for k in range(SHARE):
                        sp.dma_start(of(bytes_A, b * T + hh * SHARE + k), tile_of(A, hh * SHARE + k)).then_inc(bytes_out, 16)
                        sp.dma_start(of(bytes_AT, b * T + hh * SHARE + k), tile_of(AT, hh * SHARE + k)).then_inc(bytes_out, 16)
                if not alone:
                    restore(b, b)
                exponentials(LB, 1, b)
                sp.dma_start(Rb[:, 0, :], rrows[1, 0, :].partition_broadcast(P)).then_inc(S[LB]["rin0"], 16)
                plain(sp)
                sp.wait_ge(ln[1]["h"], b * T + T)
                sp.dma_start(of(h1, b), flat(Hn)).then_inc(x1_out, 16)
                sp.dma_start(of(x1, b), flat(X)).then_inc(x1_out, 16)
                if not alone:
                    plain(sp)
                    sp.wait_ge(maxima, b)
                    settle(sp)
                sp.dma_start(table[1:N + 1, :].rearrange("(t p) f -> p t f", p=P), Hn[:, :, :]).then_inc(tab_in, 16)
                plain(sp)
                sp.wait_ge(tab_in, b * 16 + 16)
                sp.wait_ge(x1_out, b * 32 + 32)
                sp.wait_ge(bytes_out, b * (2 * T * 16) + 2 * T * 16)
                settle(sp)

            def restore(after, latest):
                plain(sp)
                sp.wait_ge(out_done, after * 16)
                sp.wait_ge(S[LA]["pe"], latest * (LA.H * T) + LA.H * T + free_P[LA])
                settle(sp)
                sp.dma_start(flat(Hn2), of(h1, after - 1)).then_inc(x1_in, 16)
                sp.dma_start(flat(X2), of(x1, after - 1)).then_inc(x1_in, 16)

            def second(b, alone):
                if alone:
                    restore(b + 1, b)
                with sp.Fori(0, T) as t:
                    sp.dma_start(tile_of(AT, t), of(bytes_AT, b * T + t)).then_inc(AT_in, 16)
                exponentials(LC, 2, b)
                with sp.Fori(0, LC.H // 2) as hh:
                    head_rows(LC, 2, b, hh)
                plain(sp)
                sp.wait_ge(S[LC]["p"], b * (LC.H * T) + LC.H * T + P0[LC])
                settle(sp)
                with sp.Fori(0, T) as t:
                    sp.dma_start(tile_of(AT, t), of(bytes_A, b * T + t)).then_inc(A_in, 16)

            def last_layer(b, following, alone):
                if following is not None:
                    plain(sp)
                    sp.wait_ge(S[LC]["pe"], b * (LC.H * T) + LC.H * T + free_P[LC])
                    settle(sp)
                    load(following, False)
                plain(sp)
                sp.wait_ge(x_done, b + 1)
                sp.dma_start(out[bass.ds(b, 1)].rearrange("o (t p) f -> p (o t) f", p=P), X2[:, :, :]).then_inc(out_done, 16)

            sp.sem_inc(out_done, 16)
            pipeline(sp, load, first, second, last_layer)
            sp.wait_ge(out_done, B * 16 + 16)

        @block.gpsimd
        def _(pool):
            built = [0]

            def c(ins):
                built[0] += 1
                ins.then_inc(cchain, 1)
                pool.wait_ge(cchain, built[0])

            c(pool.memset(ones[:, :], 1.0))
            c(pool.memset(shiftq[:, :], GQ))
            c(pool.memset(shiftd[:, :], GD))
            c(pool.memset(eps[:, :], EPS))
            c(pool.memset(zero_row[:, :], 0.0))
            c(pool.memset(base[:, :], 0.0))
            c(pool.affine_select(out=ident[:, :], in_=ones[:, :], compare_op=ALU.is_equal, fill=0.0, base=0,
                                 pattern=[[-1, P]], channel_multiplier=1))
            c(pool.affine_select(out=before[:, :], in_=ones[0:T, 0:T + 1], compare_op=ALU.is_gt, fill=0.0, base=0,
                                 pattern=[[1, T + 1]], channel_multiplier=-1))
            c(pool.tensor_copy(identb[:, :], ident[:, :]))
            c(pool.affine_select(out=offdiag[:, :], in_=ones[:, :], compare_op=ALU.not_equal, fill=0.0, base=0,
                                 pattern=[[-1, P]], channel_multiplier=1))
            numbers = Rb[:, 0, :].bitcast(I32)
            c(pool.iota(numbers, [[1, N]], base=1, channel_multiplier=0))
            c(pool.tensor_copy(iota[:, :], numbers))
            c(pool.iota(tmpi[:, :], [[P, T]], base=1, channel_multiplier=1))
            pool.tensor_copy(selfidx[:, :], tmpi[:, :]).then_inc(consts, 1)

            def greater(v, a, b):
                v(pool.tensor_tensor(b, b, a, ALU.subtract))
                settle(pool)
                v(pool.tensor_scalar(b, b, 0.0, None, ALU.max))
                v(pool.tensor_tensor(a, a, b, ALU.add))

            def rows_of(r, slot, dst):
                plain(pool)
                pool.wait_ge(list_in, r * 16 + 32)
                pool.dma_start(idx[:, slot, :], lists[bass.ds(r, 1)].rearrange("o p k -> (o p) k")).then_inc(idx_in, 16)
                plain(pool)
                pool.wait_ge(idx_in, r * 16 + 16)
                settle(pool)
                for k in range(KEYS):
                    pool.indirect_dma_start(
                        out=dst[:, k, :], out_offset=None, in_=table,
                        in_offset=bass.IndirectOffsetOnAxis(ap=idx[:, slot, k:k + 1], axis=0)).then_inc(got[k], 16)

            def gather(b):
                plain(pool)
                pool.wait_ge(tab_in, b * 16 + 16)
                settle(pool)
                with pool.Fori(0, T) as t:
                    lo = pool.value_load(cum[0:1, bass.ds(b * (T + 1) + t, 1)], min_val=0, max_val=ROUNDS)
                    hi = pool.value_load(cum[0:1, bass.ds(b * (T + 1) + t + 1, 1)], min_val=0, max_val=ROUNDS)
                    rows_of(lo, 0, best)
                    pool.sem_inc(merged, 3)
                    with pool.Fori(lo + 1, hi) as r:
                        rows_of(r, 1, G)
                        plain(pool)
                        for k in range(KEYS):
                            pool.wait_ge(got[k], r * 16 + 16)
                        v = Chain(pool, merged, r * 3, 3)
                        greater(v, best[:, :, :], G[:, :, :])
                        v.end()
                        settle(pool)
                    v = Chain(pool, tree, (b * T + t) * TREE, TREE)
                    for width in (4, 2, 1):
                        greater(v, best[:, 0:width, :], best[:, width:2 * width, :])
                    v(pool.tensor_copy(Agg[:, bass.ds(t, 1), :].rearrange("p o f -> p (o f)"), best[:, 0, :]))
                    v.end()
                    settle(pool)
                pool.sem_inc(maxima, 1)

            gather(0)
            if B > 1:
                with pool.Fori(0, B - 1) as b:
                    plain(pool)
                    pool.wait_ge(M["sage"]["T"], b * T + T)
                    gather(b + 1)

        @block.scalar
        def _(act):
            def norm(k, b, src, dst, func):
                plain(act)
                act.wait_ge(ln[k]["v"], b * LN_CHAIN + 5)
                act.activation(small[:, 4, :], small[:, 4, :], ACT.Sqrt, bias=eps[:, 0:1], scale=1.0 / F).then_inc(ln[k]["root"], 1)
                plain(act)
                act.wait_ge(ln[k]["v"], (b + 1) * LN_CHAIN)
                with act.Fori(0, T) as t:
                    act.activation(dst[:, bass.ds(t, 1), :], src[:, bass.ds(t, 1), :], func,
                                   bias=small[:, 1, bass.ds(t, 1)], scale=small[:, 0, bass.ds(t, 1)]).then_inc(ln[k]["h"], 1)

            def prepare(L, b):
                s = S[L]
                with act.Fori(0, T // 2) as tt:
                    for u in range(2):
                        n = b * T + tt * 2 + u
                        plain(act)
                        act.wait_ge(s["T"], n + 1)
                        act.wait_ge(s["W"], n + 1)
                        act.activation(hT[:, u, 0:L.KB, :], ps[:, u, 0:L.KB * P].rearrange("p (k c) -> p k c", k=L.KB),
                                       ACT.Copy).then_inc(s["hT"], 1)
                    for u in range(2):
                        n = b * T + tt * 2 + u
                        plain(act)
                        act.wait_ge(s["W"], n + 3)
                        for k, row in enumerate((f1row, f2row)):
                            act.activation(row[0:L.H, bass.ds(tt * (2 * P) + u * P, P)],
                                           ps[0:L.H, 4 + u, k * P:(k + 1) * P], ACT.Copy).then_inc(s["row"], 1)
                plain(act)
                act.wait_ge(s["v"], b * PREP_CHAIN + 4)
                act.activation(f1row[0:L.H, :], f2row[0:L.H, :], ACT.Exp, bias=shiftq[0:L.H, 0:1], scale=1.0).then_inc(s["exp"], 1)
                plain(act)
                act.wait_ge(s["v"], b * PREP_CHAIN + 7)
                act.activation(q[:, :, 0:L.H], f2c[:, :, 0:L.H], ACT.Exp, bias=shiftq[:, 0:1], scale=1 - SLOPE).then_inc(s["exp"], 1)
                act.activation(d[:, :, 0:L.H], f2c[:, :, 0:L.H], ACT.Exp, bias=shiftd[:, 0:1], scale=SLOPE).then_inc(s["exp"], 1)
                plain(act)
                act.wait_ge(s["hs"], b + 1)
                act.activation(hsum[:, 0:L.H * L.C], ps[:, 6, 0:L.H * L.C], ACT.Copy).then_inc(s["hsc"], 1)

            def elu_exp(L, n):
                plain(act)
                act.wait_ge(S[L]["pv"], n * POST[L] + MINNED[L] + 2 * POST[L])
                E = Es if L is LA else xcbuf[:, 0:T * L.D]
                act.activation(E, E, ACT.Exp).then_inc(S[L]["e"], 1)

            def operands(m, b, results, following=None):
                with act.Fori(0, T // 2) as tt:
                    if following is not None:
                        cast(following, tt)
                    for u in range(2):
                        n = b * T + tt * 2 + u
                        plain(act)
                        act.wait_ge(M[m]["T"], n + 1)
                        act.wait_ge(M[m]["W"], n + 1)
                        act.activation(hT[:, u, :, :], ps[:, u, 0:2 * P].rearrange("p (k c) -> p k c", k=2),
                                       ACT.Copy).then_inc(M[m]["hT"], 1)
                    if results:
                        for u in range(2):
                            plain(act)
                            act.wait_ge(M[m]["W"], b * T + tt * 2 + (u + 3))
                            act.activation(Y[:, bass.ds(tt * 2 + u, 1), :],
                                           ps[:, 2 + u, 0:F].rearrange("p (o f) -> p o f", o=1), ACT.Copy).then_inc(M[m]["ev"], 1)

            def store_lists(b, t):
                lo = act.value_load(cum[0:1, bass.ds(b * (T + 1) + t, 1)], min_val=0, max_val=ROUNDS)
                hi = act.value_load(cum[0:1, bass.ds(b * (T + 1) + t + 1, 1)], min_val=0, max_val=ROUNDS)
                with act.Fori(lo, hi) as r:
                    plain(act)
                    act.wait_ge(idx_ready, r + 1)
                    act.dma_start(lists[bass.ds(r, 1)].rearrange("o p k -> (o p) k"), found_idx[:, :]).then_inc(list_in, 16)

            def cast(b, tt):
                for u in range(2):
                    n = b * T + tt * 2 + u
                    plain(act)
                    act.wait_ge(adj_in[u], (b * (T // 2) + tt + 1) * 16)
                    act.wait_ge(at_ps, n + 1)
                    act.activation(stage_bf[:, u, :], stage_i32[:, u, :],
                                   ACT.Copy, accum_out=deg[:, bass.ds(tt * 2 + u, 1)]).then_inc(bf_done, 1)
                    act.activation(A[:, bass.ds(tt * 2 + u, 1), :], stage_i32[:, u, :].rearrange("p (o n) -> p o n", o=1),
                                   ACT.Copy, scale=float(ONE8)).then_inc(cast_done, 1)

            def load(b, alone):
                with act.Fori(0, T // 2) as tt:
                    cast(b, tt)

            def first(b, alone):
                norm(0, b, X, Hn, ACT.Relu)
                prepare(LA, b)
                plain(act)
                act.wait_ge(lv, b * LV_CHAIN + LV_CHAIN)
                settle(act)
                start, count = LIST_ALL if alone else LIST_LA
                with act.Fori(0, LA.H // 2) as hh:
                    for u in range(2):
                        for k in range(count // 2):
                            store_lists(b, hh * count + (start + u * (count // 2) + k))
                        elu_exp(LA, b * LA.H + hh * 2 + u)
                prepare(LB, b)
                if not alone:
                    store_lists(b, LIST_LB)
                elu_exp(LB, b)
                norm(1, b, X, Hn, ACT.Relu)

            def second(b, alone):
                operands("sage", b, False)
                norm(4, b, Y, Y, ACT.Identity)
                norm(2, b, X2, Hn2, ACT.Relu)
                prepare(LC, b)
                if not alone:
                    start, count = LIST_LC
                    with act.Fori(0, LC.H // 2) as hh:
                        for k in range(count):
                            store_lists(b + 1, hh * count + (start + k))

            def last_layer(b, following, alone):
                norm(3, b, X2, Hn2, ACT.Relu)
                plain(act)
                act.wait_ge(ln[3]["h"], b * T + T)
                act.activation(PS3[:, :, 0:F], Hn2[:, :, :], ACT.Copy).then_inc(part, 1)
                for k in (1, 2):
                    plain(act)
                    act.wait_ge(rest_done, b * 2 + k)
                    act.activation(PS3[:, :, k * F:(k + 1) * F], rest, ACT.Copy).then_inc(part, 1)
                if not alone:
                    store_lists(b + 1, LIST_L3)
                plain(act)
                act.wait_ge(part, b * 3 + 3)
                operands("pool", b, True, following)

            act.sem_inc(cast_done, 2)
            for L in (LA, LB, LC):
                act.sem_inc(S[L]["hT"], 2)
                act.sem_inc(S[L]["row"], 4)
            for m in ("sage", "pool"):
                act.sem_inc(M[m]["hT"], 2)
            act.sem_inc(M["pool"]["ev"], 2)
            act.sem_inc(list_in, 16)
            act.wait_ge(ready, 1)
            pipeline(act, load, first, second, last_layer)

        @block.vector
        def _(dve):
            def statistics(k, b, src):
                settle(dve)
                with dve.Fori(0, T) as t:
                    dve.bn_stats(stats[:, bass.ds(t, 1), :].rearrange("p o c -> p (o c)"),
                                 src[:, bass.ds(t, 1), :].rearrange("p o c -> p (o c)")).then_inc(ln[k]["st"], 1)
                plain(dve)
                dve.wait_ge(ln[k]["st"], (b + 1) * T)
                v = Chain(dve, ln[k]["v"], b * LN_CHAIN, LN_CHAIN)
                mean_e, m2_e, mean_o, m2_o = (stats[:, :, i] for i in (1, 2, 4, 5))
                v(dve.tensor_tensor(small[:, 2, :], mean_e, mean_o, ALU.add))
                v(dve.tensor_tensor(small[:, 3, :], mean_e, mean_o, ALU.subtract))
                v(dve.tensor_tensor(small[:, 4, :], m2_e, m2_o, ALU.add))
                v(dve.scalar_tensor_tensor(small[:, 3, :], small[:, 3, :], F / 4, small[:, 3, :], ALU.mult, ALU.mult))
                v(dve.tensor_tensor(small[:, 4, :], small[:, 4, :], small[:, 3, :], ALU.add))
                plain(dve)
                dve.wait_ge(ln[k]["root"], b + 1)
                v(dve.reciprocal(small[:, 0, :], small[:, 4, :]))
                v(dve.scalar_tensor_tensor(small[:, 1, :], small[:, 2, :], -0.5, small[:, 0, :], ALU.mult, ALU.mult))
                v.end()

            def prepare(L, b):
                s, wh = S[L], WH(L)
                settle(dve)
                with dve.Fori(0, T // 2) as tt:
                    for u in range(2):
                        n = b * T + tt * 2 + u
                        plain(dve)
                        dve.wait_ge(s["W"], n + 3)
                        dve.tensor_copy(wh[:, bass.ds(tt * 2 + u, 1), :, 0:L.D].rearrange("p o h d -> p (o h) d"),
                                        ps[:, 2 + u, 0:L.H * L.D].rearrange("p (h d) -> p h d", h=L.H)).then_inc(s["ev"], 1)
                        dve.tensor_copy(f2c[:, bass.ds(tt * 2 + u, 1), 0:L.H].rearrange("p o h -> p (o h)"),
                                        ps[:, 2 + u, L.H * L.D:L.H * L.D + L.H]).then_inc(s["ev"], 1)
                v = Chain(dve, s["v"], b * PREP_CHAIN, PREP_CHAIN)
                plain(dve)
                dve.wait_ge(s["row"], (b + 1) * 2 * T + 4)
                v(dve.tensor_reduce(cmax[0:L.H, :], f2row[0:L.H, :], AX, ALU.max))
                v(dve.tensor_scalar(cdiag[0:L.H, 0:L.H], ident[0:L.H, 0:L.H], cmax[0:L.H, 0:1], None, ALU.mult))
                v(dve.tensor_scalar(f1row[0:L.H, :], f1row[0:L.H, :], cmax[0:L.H, 0:1], -(1 - SLOPE), ALU.add, ALU.mult))
                v(dve.tensor_scalar(f2row[0:L.H, :], f1row[0:L.H, :], 0.0, None, ALU.min))
                plain(dve)
                dve.wait_ge(s["ev"], (b + 1) * 2 * T + 4)
                v(dve.memset(wh[:, :, :, L.D:L.C], 1.0))
                v(dve.tensor_reduce(hpart[:, 0:L.H * L.C], wh.rearrange("p t h c -> p (h c) t"), AX, ALU.add))
                plain(dve)
                dve.wait_ge(s["cb"], b + 1)
                v(dve.tensor_tensor(f2c[:, :, 0:L.H], f2c[:, :, 0:L.H],
                                    ps[:, 7, 0:L.H].rearrange("p (o h) -> p o h", o=1).broadcast_to([P, T, L.H]), ALU.subtract))
                plain(dve)
                dve.wait_ge(s["exp"], b * 3 + 3)
                v(dve.tensor_tensor(wh, wh, d[:, :, 0:L.H].rearrange("p t (h o) -> p t h o", o=1).broadcast_to([P, T, L.H, L.C]),
                                    ALU.mult))
                v.end()
                plain(dve)
                dve.wait_ge(s["hsc"], b + 1)

            def weigh(L, slot, loaded, h, hn, between=()):
                after = dict(between)
                s = S[L]
                plain(dve)
                dve.wait_ge(s[f"rin{slot}"], loaded)
                for jb in range(T):
                    plain(dve)
                    dve.wait_ge(s["pe"], hn * T + (jb + 1))
                    dve.scalar_tensor_tensor(tiles_P[L][jb % free_P[L]], Rb[:, slot, :], q[:, jb, h], AT[:, jb, :],
                                             ALU.max, ALU.mult).then_inc(s["p"], 1)
                    if jb in after:
                        after[jb]()

            def finish(L, slot, h, hn, lone):
                s, C = S[L], L.C
                v = Chain(dve, s["pv"], (hn + 2) * POST[L], POST[L])
                Z = Pflat[:, 0:T * C] if L is LB else Zs[:, 0:T * C]
                E = (xcbuf[:, 0:T * L.D] if L is LB else Es).rearrange("p (t c) -> p t c", c=L.D)
                zt = Z.rearrange("p (t c) -> p t c", c=C)
                o = zt[:, :, 0:L.D]
                hs = hsum[:, 0:C] if L is LB else hsum[:, bass.ds(h * C, C)]
                plain(dve)
                dve.wait_ge(s["pe"], (hn + 1) * T + free_P[L])
                v(dve.tensor_tensor(zt, lone[:, :].rearrange("p (t o) -> p t o", o=1).broadcast_to([P, T, C]),
                                    hs.rearrange("p (o c) -> p o c", o=1).broadcast_to([P, T, C]), ALU.mult))
                if L is LB:
                    full, w = T // L.per_bank, L.per_bank * C
                    zf = Z[:, 0:full * w].rearrange("p (b c) -> p b c", b=full)
                    v(dve.tensor_tensor(zf, zf, ps[:, 0:full, 0:w], ALU.add))
                    v(dve.tensor_tensor(Z[:, full * w:], Z[:, full * w:], ps[:, full, 0:T * C - full * w], ALU.add))
                else:
                    acc = ps[:, 4 * slot:4 * slot + 4, :].rearrange("p b (t c) -> p (b t) c", c=L.width)[:, :, 0:C]
                    v(dve.tensor_tensor(zt, zt, acc, ALU.add))
                v(dve.reciprocal(rden[:, :], zt[:, :, L.D]))
                v(dve.tensor_tensor(o, o, rden[:, :].rearrange("p (t o) -> p t o", o=1).broadcast_to([P, T, L.D]), ALU.mult))
                if L is LC:
                    xs = X2[:, :, h * L.D:(h + 1) * L.D] if isinstance(h, int) else X2[:, :, bass.ds(h * L.D, L.D)]
                    v(dve.tensor_tensor(xs, xs, o, ALU.add))
                else:
                    v(dve.tensor_scalar(E, o, 0.0, None, ALU.min))
                    plain(dve)
                    dve.wait_ge(s["e"], hn + 1)
                    v(dve.scalar_tensor_tensor(E, o, 0.0, E, ALU.max, ALU.add))
                    if L is LA:
                        v(dve.tensor_scalar(xc[:, :, bass.ds(h * L.D, L.D)], E, -1.0, None, ALU.add))
                    else:
                        v(dve.scalar_tensor_tensor(Hn[:, :, :], E, -1.0, Hn[:, :, :], ALU.add, ALU.add))
                        v(dve.tensor_tensor(X[:, :, :], X[:, :, :], Hn[:, :, :], ALU.add))
                v.end()

            def heads(L, b, lone, lists=None):
                def head(h, pair, u, ended):
                    beside = []
                    if ended is not None:
                        beside.append((END_AT, lambda: finish(L, 1 - u, ended, b * L.H + ended, lone)))
                    if lists:
                        graph, start, count = lists
                        share = range(count // 2) if u == 0 else range(count // 2, count)
                        beside += list_tiles(graph, [pair * count + (start + k) for k in share], END_AT + 1)
                    weigh(L, u, (b * (L.H // 2) + pair + 1) * 16, slice(h, h + 1) if isinstance(h, int) else bass.ds(h, 1), b * L.H + h, beside)

                head(0, 0, 0, None)
                settle(dve)
                with dve.Fori(0, L.H // 2 - 1) as hh:
                    head(hh * 2 + 1, hh, 1, hh * 2)
                    head(hh * 2 + 2, hh + 1, 0, hh * 2 + 1)
                head(L.H - 1, L.H // 2 - 1, 1, L.H - 2)
                finish(L, 1, L.H - 1, b * L.H + L.H - 1, lone)

            def list_tiles(b, tiles, begin):
                parts = [part for t in tiles for part in list_tile(b, t)]
                return [(begin + k * (T - 1 - begin) // (len(parts) - 1), part) for k, part in enumerate(parts)]

            def list_tile(b, t):
                lo = []

                def number(t):
                    settle(dve)
                    return dve.value_load(cum[0:1, bass.ds(b * (T + 1) + t, 1)], min_val=0, max_val=ROUNDS)

                def keys():
                    v = Chain(dve, keyed, (b * T + t) * 3, 3)
                    v(dve.scalar_tensor_tensor(key[:, 0:N], A[:, bass.ds(t, 1), :].rearrange("p o n -> p (o n)"), 0.0, iota[:, :],
                                               ALU.is_gt, ALU.mult))
                    block_keys = key[:, bass.ds(t * P, P)]
                    v(dve.tensor_tensor(block_keys, block_keys, offdiag[:, :], ALU.mult))
                    v(dve.tensor_copy(key[:, N:N + 1], selfkey[:, bass.ds(t, 1)]))
                    v.end()
                    dve.sem_inc(removed, 1)

                def first_round():
                    lo.append(number(t))
                    greatest(lo[0])

                def other_rounds():
                    with dve.Fori(lo[0] + 1, number(t + 1)) as r:
                        dve.match_replace(key[:, :], keys8[:, :], key[:, :], 0.0).then_inc(removed, 1)
                        plain(dve)
                        dve.wait_ge(removed, r + 1)
                        greatest(r)

                return keys, first_round, other_rounds

            def greatest(r):
                settle(dve)
                dve.max(keys8[:, :], key[:, :]).then_inc(found, 1)
                plain(dve)
                dve.wait_ge(found, r + 1)
                dve.wait_ge(list_in, r * 16 + 16)
                dve.tensor_copy(found_idx[:, :], keys8[:, :]).then_inc(idx_ready, 1)
                plain(dve)
                dve.wait_ge(idx_ready, r + 1)
                settle(dve)

            dve.wait_ge(consts, 1)
            dve.wait_ge(w_in, LOADS * 16)
            folded = [0]

            def f(ins):
                folded[0] += 1
                ins.then_inc(w_fold, 1)
                dve.wait_ge(w_fold, folded[0])

            prod = Hn[:, :, :].rearrange("p t f -> p (t f)")
            for L, av in ((LA, Pbuf[:, 0, 0:2 * HIDDEN].rearrange("p (h e d) -> p h e d", h=LA.H, e=2)),
                          (LB, Pbuf[:, 1, 0:2 * F].rearrange("p (h e d) -> p h e d", h=1, e=2)),
                          (LC, Pbuf[:, 1, 512:512 + 2 * LC.D].rearrange("p (h e d) -> p h e d", h=1, e=2))):
                w = Wf[L]
                for k in range(L.KB):
                    for e, dst in ((0, w["f1"]), (1, w["f2"])):
                        wv = w["cat"][:, k, 0:L.H * L.D].rearrange("p (h d) -> p h d", h=L.H)
                        pv = prod[:, 0:L.H * L.D].rearrange("p (h d) -> p h d", h=L.H)
                        vec = av[:, :, e, :] if L is not LC else av[:, 0:1, e, :].broadcast_to([P, L.H, L.D])
                        f(dve.tensor_tensor(pv, wv, vec, ALU.mult))
                        f(dve.tensor_reduce(dst[:, k, :], pv, AX, ALU.add))
                    f(dve.tensor_copy(w["cat"][:, k, L.H * L.D:], w["f2"][:, k, :]))
            f(dve.tensor_tensor(rowsb[:, 0, :], rowsb[:, 0, :], rowsb[:, 1, :], ALU.add))
            f(dve.memset(WHbuf[:, T * LA.H * LA.C:], 0.0))
            for L in (LA, LB, LC):
                dve.sem_inc(S[L]["ev"], 4)
                dve.sem_inc(S[L]["pv"], 2 * POST[L])
                if P0[L]:
                    dve.sem_inc(S[L]["p"], P0[L])
            dve.sem_inc(at_done, 2)
            f(dve.memset(key[:, N:KW], 0.0))
            f(dve.memset(lone[:, :], 0.0))
            f(dve.memset(cumf[:, :], 0.0))
            dve.sem_inc(M["sage"]["ev"], 2)
            dve.sem_inc(pool_v, 2 * POOL_CHAIN)
            dve.memset(keys8[:, :], 0.0).then_inc(ready, 1)
            dve.wait_ge(ready, 1)

            def take(b, tt):
                for u in range(2):
                    n = b * T + tt * 2 + u
                    plain(dve)
                    dve.wait_ge(at_ps, n + 3)
                    dve.tensor_scalar(AT[:, :, bass.ds(tt * (2 * P) + u * P, P)],
                                      psb[:, 3, :].rearrange("p (j i) -> p j i", j=T), float(ONE8), None,
                                      ALU.mult).then_inc(at_done, 1)
                    plain(dve)
                    dve.wait_ge(cast_done, n + 3)
                    dve.scalar_tensor_tensor(Dg[:, bass.ds(tt * 2 + u, 1), :].rearrange("p o c -> p (o c)"),
                                             A[:, bass.ds(tt * 2 + u, 1), bass.ds(tt * (2 * P) + u * P, P)].rearrange("p o c -> p (o c)"),
                                             0.0, identb[:, :], ALU.is_gt, ALU.mult).then_inc(dg_done, 1)

            def load(b, alone):
                with dve.Fori(0, T // 2) as tt:
                    take(b, tt)

            def first(b, alone):
                plain(dve)
                dve.wait_ge(x_in, (b + 1) * T * 16)
                statistics(0, b, X)
                v = Chain(dve, lv, b * LV_CHAIN, LV_CHAIN)
                plain(dve)
                dve.wait_ge(dg_done, (b + 1) * T)
                v(dve.tensor_copy(lone_before[:, :], lone[:, :]))
                v(dve.tensor_reduce(aii[:, :], Dg, AX, ALU.add))
                v(dve.tensor_scalar(lone[:, :], deg[:, :], 0.0, None, ALU.is_equal))
                v(dve.tensor_tensor(aii[:, :], deg[:, :], aii[:, :], ALU.subtract))
                v(dve.scalar_tensor_tensor(selfkey[:, :], aii[:, :], 0.0, selfidx[:, :], ALU.is_equal, ALU.mult))
                plain(dve)
                dve.wait_ge(deg_ps, b + 1)
                v(dve.tensor_reduce(mdeg[:, 0:1], ps[0:T, 6, 0:P], AX, ALU.max))
                v(dve.tensor_scalar(mdegi[:, 0:1], mdeg[:, 0:1], float(KEYS - 1), None, ALU.add))
                v(dve.tensor_scalar(mdegi[:, 1:2], mdegi[:, 0:1], 3, None, ALU.arith_shift_right))
                v(dve.tensor_scalar(mdeg[:, 1:2], mdegi[:, 1:2], 2.0, None, ALU.max))
                prepare(LA, b)
                plain(dve)
                dve.wait_ge(cum_ps, b + 1)
                v(dve.tensor_scalar(cumf[:, :], ps[0:1, 5, 0:T + 1], base[:, 0:1], None, ALU.add))
                v(dve.tensor_copy(cum[:, bass.ds(b * (T + 1), T + 1)], cumf[:, :]))
                v(dve.tensor_copy(base[:, :], cumf[:, T:T + 1]))
                v.end()
                if not (alone or (isinstance(b, int) and b == 1)):
                    plain(dve)
                    dve.wait_ge(out_done, b * 16)
                heads(LA, b, lone, (b, *(LIST_ALL if alone else LIST_LA)))
                prepare(LB, b)
                weigh(LB, 0, (b + 1) * 16, slice(0, 1), b, () if alone else list_tiles(b, [LIST_LB], 1))
                finish(LB, 0, 0, b, lone)

                statistics(1, b, X)

            def second(b, alone):
                with dve.Fori(0, T // 2) as tt:
                    for u in range(2):
                        plain(dve)
                        dve.wait_ge(M["sage"]["W"], b * T + tt * 2 + (u + 3))
                        dve.tensor_tensor(Y[:, bass.ds(tt * 2 + u, 1), :].rearrange("p o f -> p (o f)"), ps[:, 2 + u, 0:F],
                                          rowsb[:, 0, :], ALU.add).then_inc(M["sage"]["ev"], 1)
                plain(dve)
                dve.wait_ge(M["sage"]["ev"], (b + 1) * T + 2)
                statistics(4, b, Y)
                v = Chain(dve, M["sage"]["y"], b * 3, 3)
                plain(dve)
                dve.wait_ge(x1_in, (b + 1) * 32)
                dve.wait_ge(ln[4]["h"], (b + 1) * T)
                for op, row in ((ALU.mult, 2), (ALU.add, 3)):
                    v(dve.tensor_tensor(Y, Y,
                                        rowsb[:, row:row + 1, :].broadcast_to([P, T, F]), op))
                v(dve.scalar_tensor_tensor(X2[:, :, :], Y, 0.0, X2[:, :, :], ALU.max, ALU.add))
                v.end()

                statistics(2, b, X2)
                prepare(LC, b)
                plain(dve)
                dve.wait_ge(AT_in, (b + 1) * (T * 16))
                plain(dve)
                dve.wait_ge(x1_out, (b + (1 if alone else 2)) * 32)
                if alone:
                    heads(LC, b, lone)
                else:
                    heads(LC, b, lone_before, (b + 1, *LIST_LC))

            def last_layer(b, following, alone):
                statistics(3, b, X2)
                dve.memset(PS3[:, :, 3 * F:SP3], 1.0).then_inc(ones3, 1)
                plain(dve)
                dve.wait_ge(part, b * 3 + 1)
                dve.tensor_tensor(rest, Hn2[:, :, :], PS3[:, :, 0:F], ALU.subtract).then_inc(rest_done, 1)
                plain(dve)
                dve.wait_ge(part, b * 3 + 2)
                dve.tensor_tensor(rest, rest, PS3[:, :, F:2 * F], ALU.subtract).then_inc(rest_done, 1)
                if not alone:
                    for work in list_tile(b + 1, LIST_L3):
                        work()
                with dve.Fori(0, T // 2) as tt:
                    for u in range(2):
                        n = b * T + tt * 2 + u
                        plain(dve)
                        dve.wait_ge(pool_ps, n + 1)
                        v = Chain(dve, pool_v, (n + 2) * POOL_CHAIN, POOL_CHAIN)
                        v(dve.tensor_scalar(count[:, u, :], ps[:, 4 + u, 3 * F:3 * F + 1], 1.0, None, ALU.max))
                        v(dve.reciprocal(count[:, u, :], count[:, u, :]))
                        v(dve.tensor_reduce(pooled[:, u, :], ps[:, 4 + u, 0:3 * F].rearrange("p (k f) -> p f k", k=3), AX, ALU.add))
                        v(dve.tensor_scalar(pooled[:, u, :], pooled[:, u, :], count[:, u, :], None, ALU.mult))
                        v.end()
                    if following is not None:
                        take(following, tt)
                v = Chain(dve, M["pool"]["y"], b, 1)
                plain(dve)
                dve.wait_ge(M["pool"]["ev"], (b + 1) * T + 2)
                v(dve.scalar_tensor_tensor(Y, Y, SLOPE3, Y, ALU.mult, ALU.max))
                dve.tensor_tensor(X2[:, :, :], X2[:, :, :], Y, ALU.add).then_inc(x_done, 1)

            pipeline(dve, load, first, second, last_layer)

        @block.tensor
        def _(pe):
            def prepare(L, b, source, arrived):
                s, w = S[L], Wf[L]
                W = L.H * L.D + L.H
                if not arrived:
                    plain(pe)
                    pe.wait_ge(S[LA]["pv"], ((b + 1) * LA.H + 2) * POST[LA])
                for tt in range(T // 2):
                    for u in range(2):
                        n = b * T + tt * 2 + u
                        plain(pe)
                        if arrived:
                            pe.wait_ge(arrived, n + 1)
                        pe.wait_ge(s["hT"], n + 1)
                        for k in range(L.KB):
                            ins = pe.transpose(ps[:, u, k * P:(k + 1) * P],
                                               source[:, tt * 2 + u, k * P:(k + 1) * P],
                                               ident[:, :])
                        ins.then_inc(s["T"], 1)
                    for u in range(2):
                        n = b * T + tt * 2 + u
                        plain(pe)
                        pe.wait_ge(s["hT"], n + 3)
                        pe.wait_ge(s["ev"], n * 2 + 2)
                        pe.wait_ge(s["row"], n * 2 + 2)
                        for k in range(L.KB):
                            pe.matmul(ps[:, 2 + u, 0:W], hT[:, u, k, :], w["cat"][:, k, :], start=k == 0, stop=k == L.KB - 1)
                        for e, wf in enumerate((w["f1"], w["f2"])):
                            for k in range(L.KB):
                                ins = pe.matmul(ps[0:L.H, 4 + u, e * P:(e + 1) * P], wf[:, k, :], hT[:, u, k, :],
                                                start=k == 0, stop=k == L.KB - 1)
                        ins.then_inc(s["W"], 1)
                plain(pe)
                pe.wait_ge(s["v"], b * PREP_CHAIN + 2)
                pe.matmul(ps[:, 7, 0:L.H], ones[0:L.H, :], cdiag[0:L.H, 0:L.H], start=True, stop=True).then_inc(s["cb"], 1)
                plain(pe)
                pe.wait_ge(s["v"], b * PREP_CHAIN + 6)
                pe.matmul(ps[:, 6, 0:L.H * L.C], ones[:, :], hpart[:, 0:L.H * L.C], start=True, stop=True).then_inc(s["hs"], 1)

            def sums(L, bank, h, hn):
                s = S[L]
                if L is not LB:
                    plain(pe)
                    pe.wait_ge(s["pv"], hn * POST[L] + ACC_READ)
                for jb in range(T):
                    plain(pe)
                    pe.wait_ge(s["p"], hn * T + (jb + 1 + P0[L]))
                    rhs = WHbuf[:, bass.ds(h * L.C + jb * L.H * L.C, L.width)]
                    for i in range(T):
                        c0 = i % L.per_bank * L.width
                        ins = pe.matmul(ps[:, bank + i // L.per_bank, c0:c0 + L.width], tiles_P[L][jb % free_P[L]][:, i * P:(i + 1) * P], rhs,
                                        start=(jb == 0 and i % L.per_bank == 0), stop=(jb == T - 1), skip_group_check=True)
                    ins.then_inc(s["pe"], 1)

            def heads(L, b):
                plain(pe)
                pe.wait_ge(S[L]["v"], (b + 1) * PREP_CHAIN)
                settle(pe)
                with pe.Fori(0, L.H // 2) as hh:
                    for u in range(2):
                        sums(L, 4 * u, hh * 2 + u, b * L.H + hh * 2 + u)

            def square(m, b, weights, following=None):
                s = M[m]
                for tt in range(T // 2):
                    if m == "pool":
                        for u in range(2):
                            n = b * T + tt * 2 + u
                            plain(pe)
                            pe.wait_ge(pool_v, n * POOL_CHAIN + POOL_CHAIN)
                            settle(pe)
                            for k in range(T):
                                ins = pe.matmul(ps[:, 4 + u, 0:3 * F + 1],
                                                A8[:, k, (tt * 2 + u) * P:(tt * 2 + u + 1) * P],
                                                PS3[:, k, 0:3 * F + 1], start=k == 0, stop=k == T - 1)
                            ins.then_inc(pool_ps, 1)
                        if following is not None:
                            transposed(following, tt)
                    for u in range(2):
                        n = b * T + tt * 2 + u
                        plain(pe)
                        pe.wait_ge(s["hT"], n + 1)
                        if m == "pool":
                            pe.wait_ge(pool_v, (n + 3) * POOL_CHAIN)
                        pe.transpose(ps[:, u, 0:P], Hn2[:, tt * 2 + u, :], ident[:, :])
                        sec = pooled[:, u, :] if m == "pool" else Agg[:, tt * 2 + u, :]
                        pe.transpose(ps[:, u, P:2 * P], sec, ident[:, :]).then_inc(s["T"], 1)
                    for u in range(2):
                        n = b * T + tt * 2 + u
                        plain(pe)
                        pe.wait_ge(s["hT"], n + 3)
                        pe.wait_ge(s["ev"], n + 1)
                        for k in range(2):
                            ins = pe.matmul(ps[:, 2 + u, 0:F], hT[:, u, k, :], weights[:, k, :], start=k == 0, stop=k == 1)
                        ins.then_inc(s["W"], 1)

            pe.sem_inc(at_ps, 2)
            for L in (LA, LB, LC):
                pe.sem_inc(S[L]["W"], 2)
                pe.sem_inc(S[L]["pe"], free_P[L])
            for m in ("sage", "pool"):
                pe.sem_inc(M[m]["W"], 2)
            pe.wait_ge(ready, 1)
            def transposed(b, tt):
                for u in range(2):
                    n = b * T + tt * 2 + u
                    plain(pe)
                    pe.wait_ge(bf_done, n + 1)
                    pe.wait_ge(at_done, n + 2)
                    for jb in range(T):
                        ins = pe.transpose(psb[:, 3, jb * P:(jb + 1) * P], stage_bf[:, u, jb * P:(jb + 1) * P], identb[:, :])
                    ins.then_inc(at_ps, 1)

            def load(b, alone):
                with pe.Fori(0, T // 2) as tt:
                    transposed(b, tt)

            def first(b, alone):
                plain(pe)
                pe.wait_ge(at_done, b * T + (T + 2))
                settle(pe)
                pe.transpose(ps[0:T, 6, 0:P], deg[:, :], ident[:, :]).then_inc(deg_ps, 1)
                prepare(LA, b, Hn, ln[0]["h"])
                plain(pe)
                pe.wait_ge(lv, b * LV_CHAIN + 9)
                settle(pe)
                pe.matmul(ps[0:1, 5, 0:T + 1], mdeg[:, 1:2], before[:, :], start=True, stop=True).then_inc(cum_ps, 1)
                heads(LA, b)
                prepare(LB, b, xc, None)
                plain(pe)
                pe.wait_ge(S[LB]["v"], (b + 1) * PREP_CHAIN)
                sums(LB, 0, 0, b)

            def second(b, alone):
                plain(pe)
                pe.wait_ge(maxima, b + 1)
                pe.wait_ge(S[LB]["pv"], (b + (2 if alone else 3)) * POST[LB] + 3)
                pe.wait_ge(x1_in, (b + 1) * 32)
                square("sage", b, Wsn)
                prepare(LC, b, Hn2, ln[2]["h"])
                heads(LC, b)

            def last_layer(b, following, alone):
                plain(pe)
                pe.wait_ge(part, (b + 1) * 3)
                pe.wait_ge(ones3, b + 1)
                pe.wait_ge(A_in, (b + 1) * (T * 16))
                square("pool", b, W3s, following)

            pipeline(pe, load, first, second, last_layer)


_INS = ["x", "adj", "L0_gnn_W1", "L0_gnn_a1", "L0_gnn_W2", "L0_gnn_a2", "L1_gnn_W_self", "L1_gnn_b_self", "L1_gnn_W_neigh",
        "L1_gnn_b_neigh", "L1_gnn_gamma", "L1_gnn_beta", "L2_gnn_W", "L2_gnn_a", "L3_gnn_W", "L3_gnn_B"]


def kernel(**inputs):
    import concourse.bacc as bacc
    import numpy as np
    from concourse.bass_utils import run_bass_kernel_spmd

    nc = bacc.Bacc("TRN2", target_bir_lowering=False, num_devices=1)
    arrays, args = {}, []
    for name in _INS:
        a = np.ascontiguousarray(inputs[name])
        arrays["in_" + name] = a
        args.append(nc.dram_tensor("in_" + name, a.shape, mybir.dt.from_np(a.dtype), kind="ExternalInput").ap())
    out = nc.dram_tensor("out", inputs["x"].shape, F32, kind="ExternalOutput").ap()
    build(nc, *args, out)
    r = run_bass_kernel_spmd(nc, [arrays], core_ids=[0])
    return r.results[0]["out"]
```
